# Optimizing a Trainium2 kernel written in Bass

```python
import numpy as np
import jax
import jax.numpy as jnp

def _softmax(x, axis=-1):
    return jax.nn.softmax(x, axis=axis)

def _gelu(x):
    return jax.nn.gelu(x, approximate=True)

def _silu(x):
    return jax.nn.silu(x)

def _sigmoid(x):
    return jax.nn.sigmoid(x)

def _layernorm(x, axis=-1, eps=1e-05):
    m = jnp.mean(x, axis=axis, keepdims=True)
    v = jnp.var(x, axis=axis, keepdims=True)
    return (x - m) / jnp.sqrt(v + eps)

def _scatter_add(tgt, idx, src, axis=0):
    return tgt.at[idx].add(src)

def _segment_sum(src, seg, n):
    return jax.ops.segment_sum(src, seg, n)
kernel_name = 'mk_sandwich_d1_jaxref_r4_0cc7bb'

def setup_inputs(seed: int=0):
    np.random.seed(seed)
    _w = jnp.asarray

    def _L0_attn_setup():
        import jax, jax.numpy as jnp
        import numpy as np
        K_FACTOR = 0.5
        key = jax.random.key(seed)
        k1, k2, k3, k4 = jax.random.split(key, 4)
        B, S, H, I = (1, 512, 1024, 2752)
        x = jax.random.normal(k1, (B, S, H), dtype=jnp.float32)
        w_gate = jax.random.normal(k2, (I, H), dtype=jnp.float32) * 0.02
        w_up = jax.random.normal(k3, (I, H), dtype=jnp.float32) * 0.02
        w_down = jax.random.normal(k4, (H, I), dtype=jnp.float32) * 0.02
        return {'x': x, 'w_gate': w_gate, 'w_up': w_up, 'w_down': w_down}
    _L0_attn_in = _L0_attn_setup()

    def _L0_ffn_setup():
        import jax, jax.numpy as jnp
        import numpy as np
        DIM = 1024
        HID = 2752
        R = 16
        SCALING = 32.0 / 16.0

        def _lora_linear(x, w, a, b):
            base = jnp.einsum('bsd,od->bso', x, w)
            low = jnp.einsum('bsr,or->bso', jnp.einsum('bsd,rd->bsr', x, a), b)
            return base + low * SCALING
        key = jax.random.key(seed)
        ks = jax.random.split(key, 10)
        s_in = 1.0 / np.sqrt(DIM)
        s_hid = 1.0 / np.sqrt(HID)
        return {'x': jax.random.normal(ks[0], (4, 512, DIM), jnp.float32), 'w1': jax.random.normal(ks[1], (HID, DIM), jnp.float32) * s_in, 'w3': jax.random.normal(ks[2], (HID, DIM), jnp.float32) * s_in, 'w2': jax.random.normal(ks[3], (DIM, HID), jnp.float32) * s_hid, 'lora_A1': jax.random.normal(ks[4], (R, DIM), jnp.float32) * s_in, 'lora_B1': jax.random.normal(ks[5], (HID, R), jnp.float32) * 0.02, 'lora_A3': jax.random.normal(ks[6], (R, DIM), jnp.float32) * s_in, 'lora_B3': jax.random.normal(ks[7], (HID, R), jnp.float32) * 0.02, 'lora_A2': jax.random.normal(ks[8], (R, HID), jnp.float32) * s_hid, 'lora_B2': jax.random.normal(ks[9], (DIM, R), jnp.float32) * 0.02}
    _L0_ffn_in = _L0_ffn_setup()
    _d = {'L0_attn_x': _L0_attn_in['x'], 'L0_attn_w_gate': _L0_attn_in['w_gate'], 'L0_attn_w_up': _L0_attn_in['w_up'], 'L0_attn_w_down': _L0_attn_in['w_down'], 'L0_ffn_w1': _L0_ffn_in['w1'], 'L0_ffn_w3': _L0_ffn_in['w3'], 'L0_ffn_w2': _L0_ffn_in['w2'], 'L0_ffn_lora_A1': _L0_ffn_in['lora_A1'], 'L0_ffn_lora_B1': _L0_ffn_in['lora_B1'], 'L0_ffn_lora_A3': _L0_ffn_in['lora_A3'], 'L0_ffn_lora_B3': _L0_ffn_in['lora_B3'], 'L0_ffn_lora_A2': _L0_ffn_in['lora_A2'], 'L0_ffn_lora_B2': _L0_ffn_in['lora_B2']}
    _x0 = _d['L0_attn_x']
    _d['L0_attn_x'] = jax.random.normal(jax.random.fold_in(jax.random.key(seed), 1), (4, 512, 1024), dtype=_x0.dtype)
    del _x0
    return _d

def reference(L0_attn_x, L0_attn_w_gate, L0_attn_w_up, L0_attn_w_down, L0_ffn_w1, L0_ffn_w3, L0_ffn_w2, L0_ffn_lora_A1, L0_ffn_lora_B1, L0_ffn_lora_A3, L0_ffn_lora_B3, L0_ffn_lora_A2, L0_ffn_lora_B2):

    def _L0_attn_ref(x, w_gate, w_up, w_down):
        import jax, jax.numpy as jnp
        import numpy as np
        K_FACTOR = 0.5
        s = jax.nn.silu(jnp.einsum('bsh,ih->bsi', x, w_gate))
        B, S, I = s.shape
        k = int(K_FACTOR * I)
        _, idx = jax.lax.top_k(-jnp.abs(s), k)
        flat = s.reshape(B * S, I)
        rows = jnp.arange(B * S)[:, None]
        flat = flat.at[rows, idx.reshape(B * S, k)].set(0.0)
        s = flat.reshape(B, S, I)
        s = s * jnp.einsum('bsh,ih->bsi', x, w_up)
        return jnp.einsum('bsi,hi->bsh', s, w_down)

    def _L0_ffn_ref(x, w1, w3, w2, lora_A1, lora_B1, lora_A3, lora_B3, lora_A2, lora_B2):
        import jax, jax.numpy as jnp
        import numpy as np
        DIM = 1024
        HID = 2752
        R = 16
        SCALING = 32.0 / 16.0

        def _lora_linear(x, w, a, b):
            base = jnp.einsum('bsd,od->bso', x, w)
            low = jnp.einsum('bsr,or->bso', jnp.einsum('bsd,rd->bsr', x, a), b)
            return base + low * SCALING
        h1 = _lora_linear(x, w1, lora_A1, lora_B1)
        h3 = _lora_linear(x, w3, lora_A3, lora_B3)
        g = jax.nn.silu(h1) * h3
        return _lora_linear(g, w2, lora_A2, lora_B2)
    x = L0_attn_x
    x = x + _layernorm(_L0_attn_ref(_layernorm(x, axis=-1), L0_attn_w_gate, L0_attn_w_up, L0_attn_w_down), axis=-1)
    x = x + _layernorm(_L0_ffn_ref(_layernorm(x, axis=-1), L0_ffn_w1, L0_ffn_w3, L0_ffn_w2, L0_ffn_lora_A1, L0_ffn_lora_B1, L0_ffn_lora_A3, L0_ffn_lora_B3, L0_ffn_lora_A2, L0_ffn_lora_B2), axis=-1)
    return x

_drawn_inputs = setup_inputs


def setup_inputs(seed=0):
    import zlib

    import numpy as np

    out = dict(_drawn_inputs(seed))
    spreads = {}
    factors = {}
    for name, (base, spread) in spreads.items():
        noise = np.random.default_rng([zlib.crc32(name.encode()), seed]).standard_normal(out[name].shape)
        drawn = base * np.exp(spread * noise) if base else spread * noise
        out[name] = jnp.asarray(drawn.astype(out[name].dtype))
    for name, factor in factors.items():
        out[name] = (out[name] * factor).astype(out[name].dtype)
    return out
```

```python
from contextlib import ExitStack

import concourse.bass as bass
from concourse import mybir
from concourse.alu_op_type import AluOpType as ALU

F32 = mybir.dt.float32
F32R = mybir.dt.float32r
U32 = mybir.dt.uint32
U8 = mybir.dt.uint8
ACT = mybir.ActivationFunctionType
AX_X = mybir.AxisListType.X

P = 128
TOKENS = 2048
H = 1024
I = 2752
R = 16
KB = H // P
NC = -(-I // P)
NP = NC // 2
NG = 4
TG = TOKENS // NG
TT = TG // P
K_ZERO = I // 2
EPS = 1e-5
Q = I // 4
GUESS = 0.75
STEPS = 8
AIM = 3.5
LORA_SCALE = 2.0
WT = H
WX = H + P

JG = NC
JU = NC + 2 * NP
JB = 1 + 2 * NC + 2 * NP + 1
JC = JG + JU + JB


def need(eng, sem, value):
    if isinstance(value, int) and value <= 0:
        return
    eng.wait_ge(sem, value)


def jobs_g(g):
    return 0 if isinstance(g, int) and g == 0 else g * JC - JB


def jobs_u(g):
    return g * JC + JG


def jobs_b(g, last):
    return g * JC + 2 * JG + JU - (JG if last else 0)


def prods_g(g):
    return 0 if isinstance(g, int) and g == 0 else g * (4 * NC + 1) - 2 * NC - 1


def prods_u(g):
    return g * (4 * NC + 1) + NC


def prods_b(g, last):
    return g * (4 * NC + 1) + (2 if last else 3) * NC


def blocks_u(g):
    return g * (16 * NP + KB) + 0


def blocks_b(g):
    return g * (16 * NP + KB) + 8 * NP


def chunks_u(g):
    return g * 2 * NC


def chunks_b(g):
    return g * 2 * NC + NC


def ffn_sandwich(nc, x, w_gate, w_up, w_down, w1, w3, w2, lora_a13, lora_b2, out):
    ctx = ExitStack()
    with ctx:
        def sb(name, shape, dt):
            return ctx.enter_context(nc.sbuf_tensor(name, shape, dt))

        def bank(name):
            return ctx.enter_context(nc.psum_tensor(name, [P, 512], F32))

        def sem(name):
            return ctx.enter_context(nc.semaphore(name))

        x_mid = nc.dram_tensor("x_mid", (TOKENS // P, P, H), F32, kind="Internal").ap()

        mag = sb("mag", [P, TT, NC * P], F32)
        sign = sb("sign", [P, NC, TG], U8)
        xa_hi = sb("xa_hi", [P, KB, TG], F32R)
        xa_lo = sb("xa_lo", [P, KB, TG], F32R)
        xb_hi = sb("xb_hi", [P, KB, TG], F32R)
        xb_lo = sb("xb_lo", [P, KB, TG], F32R)
        acc = sb("acc", [P, KB, TG], F32)
        h_hi = sb("h_hi", [P, 2, 2, TG], F32R)
        h_lo = sb("h_lo", [P, 2, 2, TG], F32R)
        raw = [sb(f"raw{i}", [P, WX], F32) for i in range(2)]
        w_hi = [sb(f"w_hi{i}", [P, WX], F32R) for i in range(2)]
        w_lo = [sb(f"w_lo{i}", [P, WX], F32R) for i in range(2)]
        hf = sb("hf", [P, 2, TG], F32)
        sm = sb("sm", [P, TG], F32)
        act_s = sb("act_s", [P, 2, TG], F32)
        row_y = sb("row_y", [P, H], F32)
        row_x = sb("row_x", [P, H], F32)
        lora_in = sb("lora_in", [P, TG], F32R)
        lora_mid = sb("lora_mid", [P, TG], F32R)
        ident = sb("ident", [P, P], F32)
        stats = sb("stats", [P, 2, 6], F32)
        mv = sb("mv", [P, 2], F32)
        ra = sb("ra", [P, 1], F32)
        rb = sb("rb", [P, 1], F32)
        rc = sb("rc", [P, 1], F32)
        cand = sb("cand", [P, TT], U32)
        kth = sb("kth", [P, TT], U32)
        bit = sb("bit", [P, TT], U32)
        below = sb("below", [P, TT], U32)
        cnt = sb("cnt", [P, TT], F32)
        quota = sb("quota", [P, TT], F32)
        at = sb("at", [P, TT], F32)
        at_old = sb("at_old", [P, TT], F32)
        cnt_old = sb("cnt_old", [P, TT], F32)
        best = sb("best", [P, TT], F32)
        best_cnt = sb("best_cnt", [P, TT], F32)
        d_at = sb("d_at", [P, TT], F32)
        d_cnt = sb("d_cnt", [P, TT], F32)
        alt = sb("alt", [P, TT], F32)
        less = sb("less", [P, TT], F32)
        flag = sb("flag", [P, TT], U32)
        tops = sb("tops", [P, 4 * 8], F32)
        top8 = sb("top8", [P, 8], F32)
        picked = sb("picked", [P, 8], F32)
        nxt = sb("nxt", [P, TT], F32)
        rank = sb("rank", [P, 8], F32)
        bad = sb("bad", [P, 32], F32)
        bad_t = sb("bad_t", [P, 32], F32)
        bad_q = sb("bad_q", [P, 1], F32)
        bad_i = sb("bad_i", [P, 1], U32)

        bank_a = [bank("bank_a0"), bank("bank_a1")]
        bank_c = [bank("bank_c0"), bank("bank_c1")]
        bank_d = [bank("bank_d0"), bank("bank_d1")]
        bank_t = bank("bank_t")
        bank_l = bank("bank_l")

        ident_ok = sem("ident_ok")
        lora_clear = sem("lora_clear")
        raw_in = [sem("raw_in0"), sem("raw_in1")]
        hi_done = sem("hi_done")
        lo_done = sem("lo_done")
        job_done = sem("job_done")
        gate_silu = sem("gate_silu")
        gate_sign = sem("gate_sign")
        gate_tr = sem("gate_tr")
        mag_done = sem("mag_done")
        masked = sem("masked")
        mask_tr = sem("mask_tr")
        sm_done = sem("sm_done")
        ffn_silu = sem("ffn_silu")
        h_done = sem("h_done")
        h_hi_done = sem("h_hi_done")
        h_lo_done = sem("h_lo_done")
        block_done = sem("block_done")
        acc_done = sem("acc_done")
        low_hi = sem("low_hi")
        low_lo = sem("low_lo")
        y_tr = sem("y_tr")
        y_copied = sem("y_copied")
        row_in = sem("row_in")
        mid_ready = sem("mid_ready")
        mid_out = sem("mid_out")
        out_ready = sem("out_ready")
        out_done = sem("out_done")
        xn_done = sem("xn_done")
        xn_tr = sem("xn_tr")
        xt_hi = sem("xt_hi")
        xt_lo = sem("xt_lo")

        x_t = x.rearrange("(n p) h -> n p h", p=P)
        out_t = out.rearrange("(n p) h -> n p h", p=P)

        def row_loads_p(g):
            return 0 if isinstance(g, int) and g == 0 else TT * (3 * g - 1)

        def row_loads_fa(g):
            return TT * (3 * g + 1)

        def row_loads_fb(g, last):
            return TT * (3 * g + 3) - (TT if last else 0)

        block = ctx.enter_context(nc.Block())

        @block.sync
        def _(sp):
            def tile(j, r, src, n):
                need(sp, lo_done, j - 1)
                sp.dma_start(raw[r][:, 0:n], src).then_inc(raw_in[r], 16)

            def phase_g(g):
                jb = jobs_g(g)
                for r in range(2):
                    tile(jb + r, r, w_gate[r], WT)
                with sp.Fori(1, NP) as q:
                    for r in range(2):
                        tile(jb + 2 * q + r, r, w_gate[2 * q + r], WT)

            def phase_u(g):
                jb = jobs_u(g)
                for r in range(2):
                    tile(jb + r, r, w_up[r], WT)
                with sp.Fori(1, NP) as p:
                    for r in range(2):
                        tile(jb + 4 * p - 2 + r, r, w_up[2 * p + r], WT)
                    for r in range(2):
                        tile(jb + 4 * p + r, r, w_down[2 * p - 2 + r], WT)
                for r in range(2):
                    tile(jb + JU - 2 + r, r, w_down[2 * NP - 2 + r], WT)

            def phase_b(g, last):
                jb = jobs_b(g, last)
                tile(jb, 0, lora_a13, WX)
                for c in range(2):
                    tile(jb + 1 + 2 * c, 1, w1[c], WX)
                    tile(jb + 2 + 2 * c, 0, w3[c], WX)
                with sp.Fori(1, NP) as p:
                    for c in range(2):
                        tile(jb + 6 * p - 1 + 2 * c, 1, w1[2 * p + c], WX)
                        tile(jb + 6 * p + 2 * c, 0, w3[2 * p + c], WX)
                    for j in range(2):
                        tile(jb + 6 * p + 3 + j, 1 - j, w2[2 * p - 2 + j], WX)
                for j in range(2):
                    tile(jb + JB - 3 + j, 1 - j, w2[2 * NP - 2 + j], WX)
                tile(jb + JB - 1, 1, lora_b2, WX)

            phase_g(0)
            phase_u(0)
            with sp.Fori(1, NG) as g:
                phase_g(g)
                phase_b(g - 1, False)
                phase_u(g)
            phase_b(NG - 1, True)

        @block.tensor
        def _(pe):
            def split_product(dst, r, at, hi, lo, first, last):
                wh, wl = w_hi[r][:, at:at + P], w_lo[r][:, at:at + P]
                nc.tensor.matmul(dst, wh, hi, start=first, stop=False)
                nc.tensor.matmul(dst, wh, lo, start=False, stop=False)
                return nc.tensor.matmul(dst, wl, hi, start=False, stop=last)

            def job_in(dst, j, r, xh, xl, lora=False):
                pe.wait_ge(lo_done, j + 1)
                for k in range(KB):
                    ins = split_product(dst, r, k * P, xh[:, k, :], xl[:, k, :], k == 0,
                                        k == KB - 1 and not lora)
                if lora:
                    nc.tensor.matmul(dst, w_hi[r][:, H:WX], lora_in[:, :], start=False, stop=False)
                    ins = nc.tensor.matmul(dst, w_lo[r][:, H:WX], lora_in[:, :], start=False, stop=True)
                ins.then_inc(job_done, 1)

            def gate_transposes(n, r):
                pe.wait_ge(gate_silu, n + 1)
                need(pe, mag_done, n)
                for t in range(TT):
                    ins = nc.tensor.transpose(bank_t[:, t * P:(t + 1) * P],
                                              act_s[:, r, t * P:(t + 1) * P], ident[:, :])
                ins.then_inc(gate_tr, 1)

            def phase_g(g):
                jb = jobs_g(g)
                n0 = g * NC

                def chunk(c, r, first):
                    if not first:
                        pe.wait_ge(gate_silu, n0 + c - 1)
                    job_in(bank_a[r][:, :], jb + c, r, xa_hi, xa_lo)

                pe.wait_ge(xt_lo, 2 * (2 * TT * g + TT))
                chunk(0, 0, True)
                chunk(1, 1, True)
                gate_transposes(n0, 0)
                with pe.Fori(1, NP) as q:
                    chunk(2 * q, 0, False)
                    gate_transposes(n0 + 2 * q - 1, 1)
                    chunk(2 * q + 1, 1, False)
                    gate_transposes(n0 + 2 * q, 0)
                gate_transposes(n0 + NC - 1, 1)

            def down_job(blocks, j, r, half, slot, p_first, y_before, lora=None):
                pe.wait_ge(lo_done, j + 1)
                if lora is not None:
                    split_product(bank_l[:, :], r, H, h_hi[:, slot, half, :], h_lo[:, slot, half, :], *lora)
                for b in range(4):
                    if p_first and half == 0 and b < 2:
                        need(pe, y_copied, y_before)
                    else:
                        pe.wait_ge(acc_done, blocks + 4 * half + b - 1)
                    for c in range(2):
                        ins = split_product(bank_d[b % 2][:, :], r, c * 512 + b * P, h_hi[:, slot, c, :],
                                            h_lo[:, slot, c, :], c == 0, c == 1)
                    ins.then_inc(block_done, 1)

            def phase_u(g):
                jb, c0, bb = jobs_u(g), g * NC, blocks_u(g)
                hb = chunks_u(g)

                def ups(p, j, first):
                    for r in range(2):
                        c = 2 * p + r
                        pe.wait_ge(masked, c0 + c + 1)
                        need(pe, sm_done, c0 + c)
                        for t in range(TT):
                            ins = nc.tensor.transpose(bank_t[:, t * P:(t + 1) * P],
                                                      act_s[:, r, t * P:(t + 1) * P], ident[:, :])
                        ins.then_inc(mask_tr, 1)
                        if not first:
                            pe.wait_ge(h_done, hb + c - 1)
                        job_in(bank_a[r][:, :], j + r, r, xa_hi, xa_lo)

                def downs(p, j, slot, p_first):
                    pe.wait_ge(h_lo_done, hb + 2 * p + 2)
                    for half in range(2):
                        down_job(bb + 8 * p, j + half, half, half, slot, p_first, 4 * TT * g)

                pe.wait_ge(gate_silu, (g + 1) * NC)
                if not (isinstance(g, int) and g == 0):
                    pe.wait_ge(ffn_silu, g * NC)
                ups(0, jb, True)
                ups(1, jb + 2, False)
                downs(0, jb + 4, 0, True)
                with pe.Fori(1, NP // 2) as m:
                    for s in range(2):
                        p = 2 * m + s
                        ups(p, jb + 4 * p - 2, False)
                        downs(p - 1, jb + 4 * p, 1 - s, False)
                ups(NP - 1, jb + 4 * NP - 6, False)
                downs(NP - 2, jb + 4 * NP - 4, 1, False)
                downs(NP - 1, jb + 4 * NP - 2, 0, False)

            def y_transposes(n, blocks):
                pe.wait_ge(acc_done, blocks)
                for t in range(TT):
                    for half in range(2):
                        need(pe, y_copied, 2 * (n + t))
                        for b in range(4):
                            ins = nc.tensor.transpose(bank_d[half][:, b * P:(b + 1) * P],
                                                      acc[:, 4 * half + b, t * P:(t + 1) * P], ident[:, :])
                        ins.then_inc(y_tr, 1)
                    yield t

            def xn_transposes(n, t):
                pe.wait_ge(xn_done, n + t + 1)
                need(pe, xt_lo, 2 * (n + t))
                for half in range(2):
                    for b in range(4):
                        k = 4 * half + b
                        ins = nc.tensor.transpose(bank_a[half][:, b * P:(b + 1) * P],
                                                  row_y[:, k * P:(k + 1) * P], ident[:, :])
                    ins.then_inc(xn_tr, 1)

            def prepare_a(g):
                for t in range(TT):
                    xn_transposes(2 * TT * g, t)

            def finish_a(g):
                for t in y_transposes(2 * TT * g, blocks_u(g) + 8 * NP):
                    xn_transposes(2 * TT * g + TT, t)

            def finish_b(g):
                for _ in y_transposes(2 * TT * g + TT, blocks_b(g) + 8 * NP + KB):
                    pass

            def phase_b(g, last):
                jb, bb, hb = jobs_b(g, last), blocks_b(g), chunks_b(g)
                n0 = g * NC
                pe.wait_ge(xt_lo, 2 * (2 * TT * g + 2 * TT))
                pe.wait_ge(gate_silu, (g + 1 if last else g + 2) * NC)
                pe.wait_ge(lo_done, jb + 1)
                need(pe, low_lo, 2 * g)
                for k in range(KB):
                    ins = split_product(bank_l[:, :], 0, k * P, xb_hi[:, k, :], xb_lo[:, k, :],
                                        k == 0, k == KB - 1)
                ins.then_inc(job_done, 1)

                def pairs(p, j, first):
                    for c in range(2):
                        if not first:
                            pe.wait_ge(ffn_silu, n0 + 2 * p + c - 1)
                        job_in(bank_a[c][:, :], j + 2 * c, 1, xb_hi, xb_lo, True)
                        if not first:
                            pe.wait_ge(h_done, hb + 2 * p + c - 1)
                        job_in(bank_c[c][:, :], j + 2 * c + 1, 0, xb_hi, xb_lo, True)

                def downs(p, j, slot, p_first, p_last=False):
                    pe.wait_ge(h_lo_done, hb + 2 * p + 2)
                    for half in range(2):
                        down_job(bb + 8 * p, j + half, 1 - half, half, slot, p_first,
                                 4 * TT * g + 2 * TT, (p_first and half == 0, p_last and half == 1))

                pe.wait_ge(low_lo, 2 * g + 1)
                pairs(0, jb + 1, True)
                pairs(1, jb + 5, False)
                downs(0, jb + 9, 0, True)
                with pe.Fori(1, NP // 2) as m:
                    for s in range(2):
                        p = 2 * m + s
                        pairs(p, jb + 6 * p - 1, False)
                        downs(p - 1, jb + 6 * p + 3, 1 - s, False)
                pairs(NP - 1, jb + 6 * NP - 7, False)
                downs(NP - 2, jb + 6 * NP - 3, 1, False)
                downs(NP - 1, jb + JB - 3, 0, False, True)
                pe.wait_ge(low_lo, 2 * g + 2)
                pe.wait_ge(lo_done, jb + JB)
                for b in range(KB):
                    pe.wait_ge(acc_done, bb + 8 * NP + b - 1)
                    nc.tensor.matmul(bank_d[b % 2][:, :], w_hi[1][:, b * P:(b + 1) * P], lora_mid[:, :],
                                     start=True, stop=False)
                    ins = nc.tensor.matmul(bank_d[b % 2][:, :], w_lo[1][:, b * P:(b + 1) * P],
                                           lora_mid[:, :], start=False, stop=True)
                    ins.then_inc(block_done, 1)

            pe.wait_ge(ident_ok, 2)
            prepare_a(0)
            phase_g(0)
            phase_u(0)
            finish_a(0)
            with pe.Fori(1, NG) as g:
                prepare_a(g)
                phase_g(g)
                phase_b(g - 1, False)
                finish_b(g - 1)
                phase_u(g)
                finish_a(g)
            phase_b(NG - 1, True)
            finish_b(NG - 1)

        @block.scalar
        def _(act):
            def w_high(j, r, n, free, value):
                need(act, free, value)
                act.wait_ge(raw_in[r], 8 * (j - r) + 16)
                nc.scalar.activation(w_hi[r][:, 0:n], raw[r][:, 0:n], ACT.Copy).then_inc(hi_done, 1)

            def h_high(n, slot, r):
                act.wait_ge(h_done, n + 1)
                nc.scalar.activation(h_hi[:, slot, r, :], hf[:, r, :], ACT.Copy).then_inc(h_hi_done, 1)

            def phase_g(g, width):
                jb, n0, pb = jobs_g(g), g * NC, prods_g(g)

                def chunk(c, r, n, first):
                    w_high(jb + c + 2, r, n, job_done, pb + c + 1)
                    if first:
                        need(act, h_done, g * 2 * NC - NC if not isinstance(g, int) else 0)
                    else:
                        act.wait_ge(gate_tr, n0 + c - 1)
                        act.wait_ge(gate_sign, n0 + c - 1)
                    nc.scalar.activation(act_s[:, r, :], bank_a[r][:, :], ACT.Silu).then_inc(gate_silu, 1)

                def magnitude(c):
                    act.wait_ge(gate_tr, n0 + c + 1)
                    nc.scalar.activation(mag[:, :, bass.ds(c * P, P)],
                                         bank_t[:, :].rearrange("p (t i) -> p t i", t=TT),
                                         ACT.Abs).then_inc(mag_done, 1)

                chunk(0, 0, WT, True)
                chunk(1, 1, WT, True)
                magnitude(0)
                with act.Fori(1, NP - 1) as q:
                    chunk(2 * q, 0, WT, False)
                    magnitude(2 * q - 1)
                    chunk(2 * q + 1, 1, WT, False)
                    magnitude(2 * q)
                chunk(NC - 2, 0, width, False)
                magnitude(NC - 3)
                chunk(NC - 1, 1, width, False)
                magnitude(NC - 2)
                magnitude(NC - 1)

            def phase_u(g):
                jb, pb, bb, hb = jobs_u(g), prods_u(g), blocks_u(g), chunks_u(g)

                def ups(p, j, slot):
                    for r in range(2):
                        w_high(j + r + 2, r, WT, job_done, pb + 2 * p + r + 1)
                        h_high(hb + 2 * p + r, slot, r)

                def downs(p, j, n):
                    for half in range(2):
                        w_high(j + half + 2, half, n, block_done, bb + 8 * p + 4 * half + 4)

                ups(0, jb, 0)
                ups(1, jb + 2, 1)
                downs(0, jb + 4, WT)
                with act.Fori(1, NP // 2) as m:
                    for s in range(2):
                        p = 2 * m + s
                        ups(p, jb + 4 * p - 2, s)
                        downs(p - 1, jb + 4 * p, WT)
                ups(NP - 1, jb + 4 * NP - 6, 0)
                downs(NP - 2, jb + 4 * NP - 4, WT)
                downs(NP - 1, jb + 4 * NP - 2, WX)

            def phase_b(g, last):
                jb, pb, bb, hb = jobs_b(g, last), prods_b(g, last), blocks_b(g), chunks_b(g)
                n0 = g * NC
                w_high(jb + 2, 0, WX, job_done, pb + 1)
                nc.scalar.activation(lora_in[:, :], bank_l[:, :], ACT.Copy, scale=LORA_SCALE).then_inc(low_hi, 1)

                def pairs(p, j, slot, first):
                    for c in range(2):
                        k = 2 * p + c
                        w_high(j + 2 * c + 2, 1, WX, job_done, pb + 2 * k + 2)
                        if first:
                            act.wait_ge(gate_sign, (g + 1 if last else g + 2) * NC)
                        else:
                            act.wait_ge(h_done, hb + k - 1)
                        nc.scalar.activation(act_s[:, c, :], bank_a[c][:, :], ACT.Silu).then_inc(ffn_silu, 1)
                        w_high(j + 2 * c + 3, 0, WX, job_done, pb + 2 * k + 3)
                        h_high(hb + k, slot, c)

                def downs(p, j, n):
                    for half in range(2):
                        w_high(j + half + 2, 1 - half, WX, block_done, bb + 8 * p + 4 * half + 4)

                pairs(0, jb + 1, 0, True)
                pairs(1, jb + 5, 1, False)
                downs(0, jb + 9, WX)
                with act.Fori(1, NP // 2) as m:
                    for s in range(2):
                        p = 2 * m + s
                        pairs(p, jb + 6 * p - 1, s, False)
                        downs(p - 1, jb + 6 * p + 3, WX)
                pairs(NP - 1, jb + 6 * NP - 7, 0, False)
                downs(NP - 2, jb + 6 * NP - 3, WX)
                w_high(jb + JB - 1, 1, WX, block_done, bb + 8 * NP - 4)
                if not last:
                    w_high(jb + JB, 0, WT, block_done, bb + 8 * NP)
                act.wait_ge(block_done, bb + 8 * NP)
                nc.scalar.activation(lora_mid[:, :], bank_l[:, :], ACT.Copy, scale=LORA_SCALE).then_inc(low_hi, 1)
                if not last:
                    w_high(jb + JB + 1, 1, WT, block_done, bb + 8 * NP + KB)

            def x_high(dst, n, t):
                for half in range(2):
                    act.wait_ge(xn_tr, 2 * (n + t) + half + 1)
                    nc.scalar.activation(dst[:, 4 * half:4 * half + 4, t * P:(t + 1) * P],
                                         bank_a[half][:, :].rearrange("p (k i) -> p k i", k=4),
                                         ACT.Copy).then_inc(xt_hi, 1)

            def y_copy(n, t):
                for half in range(2):
                    act.wait_ge(y_tr, 2 * (n + t) + half + 1)
                    nc.scalar.activation(row_y[:, half * 512:half * 512 + 512], bank_d[half][:, :],
                                         ACT.Copy).then_inc(y_copied, 1)

            def prepare_a(g):
                n = 2 * TT * g
                for t in range(TT):
                    need(act, xn_done, n + t)
                    if t == 0:
                        need(act, mid_out, 16 * TT * g)
                    act.dma_start(row_x[:, :], x_t[TT * g + t]).then_inc(row_in, 16)
                    x_high(xa_hi, n, t)

            def finish_a(g):
                n = 2 * TT * g + TT
                for t in range(TT):
                    act.wait_ge(xn_done, n + t)
                    need(act, mid_out, 16 * (TT * g + t))
                    if t == 0:
                        need(act, out_done, 16 * TT * g)
                    act.dma_start(row_x[:, :], x_t[TT * g + t]).then_inc(row_in, 16)
                    act.wait_ge(xn_tr, 2 * (n + t))
                    y_copy(2 * TT * g, t)
                    act.wait_ge(mid_ready, TT * g + t + 1)
                    act.dma_start(x_mid[TT * g + t], row_x[:, :]).then_inc(mid_out, 16)
                    x_high(xb_hi, n, t)

            def finish_b(g, last):
                for t in range(TT):
                    if t == 0:
                        before = 2 * TT * (g + 1) + (0 if last else TT)
                        act.wait_ge(xn_done, before)
                        act.wait_ge(xn_tr, 2 * before)
                        act.wait_ge(mid_out, 16 * TT * (g + 1))
                    need(act, out_done, 16 * (TT * g + t))
                    act.dma_start(row_x[:, :], x_mid[TT * g + t]).then_inc(row_in, 16)
                    need(act, out_ready, TT * g + t)
                    y_copy(2 * TT * g + TT, t)
                    act.wait_ge(out_ready, TT * g + t + 1)
                    act.dma_start(out_t[TT * g + t], row_x[:, :]).then_inc(out_done, 16)

            act.wait_ge(lora_clear, 2)
            for r in range(2):
                w_high(r, r, WT, job_done, 0)
            prepare_a(0)
            phase_g(0, WT)
            phase_u(0)
            finish_a(0)
            with act.Fori(1, NG) as g:
                prepare_a(g)
                phase_g(g, WX)
                phase_b(g - 1, False)
                finish_b(g - 1, False)
                phase_u(g)
                finish_a(g)
            phase_b(NG - 1, True)
            finish_b(NG - 1, True)
            act.wait_ge(out_done, 16 * TT * NG)
            act.wait_ge(mid_out, 16 * TT * NG)

        @block.gpsimd
        def _(pool):
            def w_low(j, r, n):
                pool.wait_ge(hi_done, j + 1)
                nc.gpsimd.tensor_tensor(w_lo[r][:, 0:n], raw[r][:, 0:n], w_hi[r][:, 0:n],
                                        ALU.subtract).then_inc(lo_done, 1)

            def h_low(n, slot, r):
                pool.wait_ge(h_hi_done, n + 1)
                nc.gpsimd.tensor_tensor(h_lo[:, slot, r, :], hf[:, r, :], h_hi[:, slot, r, :],
                                        ALU.subtract).then_inc(h_lo_done, 1)

            def phase_g(g, width):
                jb = jobs_g(g)
                with pool.Fori(0, NP - 1) as q:
                    for r in range(2):
                        w_low(jb + 2 * q + r + 2, r, WT)
                for r in range(2):
                    w_low(jb + NC + r, r, width)

            def phase_u(g):
                jb, hb = jobs_u(g), chunks_u(g)

                def ups(p, j, slot):
                    for r in range(2):
                        w_low(j + r + 2, r, WT)
                        h_low(hb + 2 * p + r, slot, r)

                def downs(j, n):
                    for half in range(2):
                        w_low(j + half + 2, half, n)

                ups(0, jb, 0)
                ups(1, jb + 2, 1)
                downs(jb + 4, WT)
                with pool.Fori(1, NP // 2) as m:
                    for s in range(2):
                        p = 2 * m + s
                        ups(p, jb + 4 * p - 2, s)
                        downs(jb + 4 * p, WT)
                ups(NP - 1, jb + 4 * NP - 6, 0)
                downs(jb + 4 * NP - 4, WT)
                downs(jb + 4 * NP - 2, WX)

            def phase_b(g, last):
                jb, hb = jobs_b(g, last), chunks_b(g)
                w_low(jb + 2, 0, WX)

                def pairs(p, j, slot):
                    for c in range(2):
                        w_low(j + 2 * c + 2, 1, WX)
                        w_low(j + 2 * c + 3, 0, WX)
                        h_low(hb + 2 * p + c, slot, c)

                def downs(j):
                    for half in range(2):
                        w_low(j + half + 2, 1 - half, WX)

                pairs(0, jb + 1, 0)
                pairs(1, jb + 5, 1)
                downs(jb + 9)
                with pool.Fori(1, NP // 2) as m:
                    for s in range(2):
                        p = 2 * m + s
                        pairs(p, jb + 6 * p - 1, s)
                        downs(jb + 6 * p + 3)
                pairs(NP - 1, jb + 6 * NP - 7, 0)
                downs(jb + 6 * NP - 3)
                w_low(jb + JB - 1, 1, WX)
                if not last:
                    w_low(jb + JB, 0, WT)
                    w_low(jb + JB + 1, 1, WT)

            nc.gpsimd.memset(ident[:, :], 0.0).then_inc(ident_ok, 1)
            pool.wait_ge(ident_ok, 1)
            nc.gpsimd.affine_select(out=ident[:, :], in_=ident[:, :], compare_op=ALU.not_equal, fill=1.0,
                                    base=0, pattern=[[-1, P]], channel_multiplier=1).then_inc(ident_ok, 1)
            for r in range(2):
                nc.gpsimd.memset(raw[r][:, WT:WX], 0.0).then_inc(lora_clear, 1)
            for r in range(2):
                w_low(r, r, WT)
            phase_g(0, WT)
            phase_u(0)
            with pool.Fori(1, NG) as g:
                phase_g(g, WX)
                phase_b(g - 1, False)
                phase_u(g)
            phase_b(NG - 1, True)

        @block.vector
        def _(dve):
            def statistics(row):
                for i in range(2):
                    nc.vector.bn_stats(stats[:, i, :], row[:, i * 512:(i + 1) * 512])
                dve.drain()
                nc.vector.bn_aggr(mv[:, :], stats[:, :, :])
                dve.drain()
                nc.vector.tensor_scalar(ra[:, :], mv[:, 1:2], EPS, None, ALU.add)
                dve.drain()
                nc.vector.tensor_scalar(rb[:, :].bitcast(mybir.dt.int32), ra[:, :].bitcast(mybir.dt.int32),
                                        -0.5, float(0x5F3759DF), ALU.mult, ALU.add)
                dve.drain()
                for _ in range(4):
                    nc.vector.tensor_scalar(rc[:, :], rb[:, :], rb[:, :], ra[:, :], ALU.mult, ALU.mult)
                    dve.drain()
                    nc.vector.tensor_scalar(rc[:, :], rc[:, :], -0.5, 1.5, ALU.mult, ALU.add)
                    dve.drain()
                    nc.vector.tensor_tensor(rb[:, :], rb[:, :], rc[:, :], ALU.mult)
                    dve.drain()

            def normalise(dst, src):
                return nc.vector.tensor_scalar(dst[:, :], src[:, :], mv[:, 0:1], rb[:, :],
                                               ALU.subtract, ALU.mult)

            def x_low(hi, lo, n, t):
                for half in range(2):
                    dve.wait_ge(xt_hi, 2 * (n + t) + half + 1)
                    s = (slice(None), slice(4 * half, 4 * half + 4), slice(t * P, (t + 1) * P))
                    nc.vector.tensor_tensor(lo[s], bank_a[half][:, :].rearrange("p (k i) -> p k i", k=4),
                                            hi[s].bitcast(F32), ALU.subtract).then_inc(xt_lo, 1)

            def prepare_a(g):
                n = 2 * TT * g
                for t in range(TT):
                    dve.wait_ge(row_in, 16 * (row_loads_p(g) + t + 1))
                    statistics(row_x)
                    need(dve, xn_tr, 2 * (n + t))
                    normalise(row_y, row_x).then_inc(xn_done, 1)
                    x_low(xa_hi, xa_lo, n, t)

            def finish_a(g):
                n = 2 * TT * g + TT
                for t in range(TT):
                    dve.wait_ge(y_copied, 2 * (2 * TT * g + t + 1))
                    statistics(row_y)
                    normalise(row_y, row_y)
                    dve.drain()
                    dve.wait_ge(row_in, 16 * (row_loads_fa(g) + t + 1))
                    nc.vector.tensor_tensor(row_x[:, :], row_x[:, :], row_y[:, :], ALU.add).then_inc(mid_ready, 1)
                    dve.drain()
                    statistics(row_x)
                    normalise(row_y, row_x).then_inc(xn_done, 1)
                    x_low(xb_hi, xb_lo, n, t)

            def finish_b(g, last):
                for t in range(TT):
                    dve.wait_ge(y_copied, 2 * (2 * TT * g + TT + t + 1))
                    statistics(row_y)
                    normalise(row_y, row_y)
                    dve.drain()
                    dve.wait_ge(row_in, 16 * (row_loads_fb(g, last) + t + 1))
                    nc.vector.tensor_tensor(row_x[:, :], row_x[:, :], row_y[:, :], ALU.add).then_inc(out_ready, 1)

            def phase_g(g):
                n0 = g * NC

                def signs(c, r):
                    dve.wait_ge(gate_silu, n0 + c + 1)
                    nc.vector.tensor_scalar(sign[:, c, :] if isinstance(c, int) else sign[:, bass.ds(c, 1), :],
                                            act_s[:, r, :] if isinstance(c, int) else act_s[:, r:r + 1, :],
                                            0.0, None, ALU.is_ge).then_inc(gate_sign, 1)

                with dve.Fori(0, NP) as q:
                    for r in range(2):
                        signs(2 * q + r, r)

            def count_below(bound, tiles=range(TT)):
                junk = [row_y[:, :].bitcast(U8)[:, 0:I], row_x[:, :].bitcast(U8)[:, 0:I]]
                for t in tiles:
                    nc.vector.tensor_scalar(junk[t % 2], mag[:, t, 0:I], bound[:, t:t + 1], None,
                                            ALU.is_lt, ALU.add, accum_out=cnt[:, t:t + 1])
                    if t % 2:
                        dve.drain()

            def search_sums(g, tiles):
                if tiles[0] == 0:
                    dve.wait_ge(mag_done, (g + 1) * NC)
                    dve.wait_ge(xn_tr, 2 * (2 * TT * g + TT))
                junk = [row_y, row_x]
                for t in tiles:
                    for i in range(4):
                        nc.vector.tensor_scalar(junk[i % 2][:, 0:Q], mag[:, t, i * Q:(i + 1) * Q], 1.0, None,
                                                ALU.mult, ALU.add, accum_out=tops[:, 4 * t + i:4 * t + i + 1])
                        if i % 2:
                            dve.drain()

            def search_start():
                nc.vector.tensor_reduce(at[:, :], tops[:, 0:4 * TT].rearrange("p (t i) -> p t i", i=4), AX_X, ALU.add)
                nc.vector.memset(at_old[:, :], 0.0)
                nc.vector.memset(cnt_old[:, :], 0.0)
                nc.vector.memset(best[:, :], 0.0)
                nc.vector.memset(best_cnt[:, :], 4.0 * I)
                dve.drain()
                nc.vector.tensor_scalar(at[:, :], at[:, :], GUESS / I, None, ALU.mult)
                dve.drain()

            def search_move():
                nc.vector.tensor_tensor(less[:, :], cnt[:, :], best_cnt[:, :], ALU.is_lt)
                nc.vector.tensor_tensor(d_cnt[:, :], cnt[:, :], cnt_old[:, :], ALU.subtract)
                nc.vector.tensor_tensor(d_at[:, :], at[:, :], at_old[:, :], ALU.subtract)
                nc.vector.tensor_scalar(alt[:, :], cnt[:, :], 1.0, None, ALU.add)
                dve.drain()
                nc.vector.scalar_tensor_tensor(flag[:, :], cnt[:, :], float(K_ZERO), less[:, :], ALU.is_ge, ALU.mult)
                nc.vector.tensor_scalar(below[:, :], d_cnt[:, :], 0.0, None, ALU.is_equal)
                dve.drain()
                nc.vector.copy_predicated(best[:, :], flag[:, :], at[:, :])
                nc.vector.copy_predicated(best_cnt[:, :], flag[:, :], cnt[:, :])
                nc.vector.copy_predicated(d_at[:, :], below[:, :], at[:, :])
                nc.vector.copy_predicated(d_cnt[:, :], below[:, :], alt[:, :])
                nc.vector.tensor_scalar(less[:, :], cnt[:, :], -1.0, K_ZERO + AIM, ALU.mult, ALU.add)
                nc.vector.tensor_copy(at_old[:, :], at[:, :])
                nc.vector.tensor_copy(cnt_old[:, :], cnt[:, :])
                dve.drain()
                nc.vector.reciprocal(alt[:, :], d_cnt[:, :])
                nc.vector.tensor_tensor(d_at[:, :], d_at[:, :], less[:, :], ALU.mult)
                dve.drain()
                nc.vector.tensor_tensor(d_at[:, :], d_at[:, :], alt[:, :], ALU.mult)
                dve.drain()
                nc.vector.tensor_tensor(at[:, :], at[:, :], d_at[:, :], ALU.add)
                dve.drain()

            def search_pick(tiles):
                for t in tiles:
                    for i in range(4):
                        part = (row_y, row_x)[i % 2][:, 0:Q]
                        m = mag[:, t, i * Q:(i + 1) * Q]
                        nc.vector.scalar_tensor_tensor(part, m, best[:, t:t + 1], m, ALU.is_lt, ALU.mult)
                        dve.drain()
                        nc.vector.max(tops[:, i * 8:(i + 1) * 8], part)
                    if t == 0:
                        nc.vector.tensor_scalar(less[:, :], best_cnt[:, :], -float(K_ZERO), None, ALU.add)
                        nc.vector.tensor_scalar(alt[:, :], best_cnt[:, :], 1.0 - K_ZERO, None, ALU.add)
                    dve.drain()
                    nc.vector.max(top8[:, :], tops[:, :])
                    dve.drain()
                    nc.vector.scalar_tensor_tensor(picked[:, :], rank[:, :], less[:, t:t + 1], top8[:, :],
                                                   ALU.is_equal, ALU.mult, accum_out=kth[:, t:t + 1].bitcast(F32))
                    dve.drain()
                    nc.vector.scalar_tensor_tensor(picked[:, :], rank[:, :], alt[:, t:t + 1], top8[:, :],
                                                   ALU.is_equal, ALU.mult, accum_out=nxt[:, t:t + 1])
                    dve.drain()

            def search_end():
                nc.vector.tensor_scalar(below[:, :], less[:, :], 0.0, None, ALU.is_equal)
                dve.drain()
                nc.vector.copy_predicated(kth[:, :], below[:, :], best[:, :].bitcast(U32))
                dve.drain()
                nc.vector.tensor_tensor(alt[:, :], nxt[:, :], kth[:, :].bitcast(F32), ALU.is_lt)
                dve.drain()
                nc.vector.scalar_tensor_tensor(alt[:, :], less[:, :], 7.5, alt[:, :], ALU.is_lt, ALU.mult)
                dve.drain()
                nc.vector.tensor_scalar(alt[:, :], alt[:, :], 1.0, None, ALU.is_lt)
                dve.drain()
                nc.vector.tensor_reduce(bad[:, 0:1], alt[:, :], AX_X, ALU.max)
                dve.drain()
                nc.vector.transpose(bad_t[:, :], bad[:, :])
                dve.drain()
                nc.vector.tensor_reduce(bad_q[:, :], bad_t[:, :], AX_X, ALU.max)
                dve.drain()
                nc.vector.tensor_copy(bad_i[:, :], bad_q[:, :])
                dve.drain()
                n = [nc.vector.value_load(bad_i[q:q + 1, 0:1], min_val=0, max_val=1) for q in range(0, P, 32)]
                with dve.If(n[0] + n[1] + n[2] + n[3] > 0):
                    search_all()
                dve.drain()

            def search_all():
                nc.vector.memset(kth[:, :], 0)
                nc.vector.memset(bit[:, :], 1 << 30)
                nc.vector.memset(cand[:, :], 1 << 30)
                dve.drain()
                with dve.Fori(0, 31):
                    count_below(cand[:, :].bitcast(F32))
                    nc.vector.tensor_scalar(below[:, :], cnt[:, :], float(K_ZERO), None, ALU.is_lt)
                    dve.drain()
                    nc.vector.copy_predicated(kth[:, :], below[:, :], cand[:, :])
                    nc.vector.tensor_scalar(bit[:, :], bit[:, :], 1, None, ALU.logical_shift_right)
                    dve.drain()
                    nc.vector.tensor_tensor(cand[:, :], kth[:, :], bit[:, :], ALU.bitwise_or)
                    dve.drain()
                count_below(kth[:, :].bitcast(F32))
                nc.vector.tensor_scalar(quota[:, :], cnt[:, :], -1.0, float(K_ZERO), ALU.mult, ALU.add)
                dve.drain()
                S = 344
                eq, cum, keep = row_y[:, 0:S], row_x[:, 0:S], row_x[:, S:2 * S]
                last = row_x[:, 2 * S:2 * S + 1]
                for t in range(TT):
                    nc.vector.memset(last, 0.0)
                    dve.drain()
                    with dve.Fori(0, I // S) as i:
                        m = mag[:, t, bass.ds(i * S, S)]
                        nc.vector.tensor_scalar(eq, m, kth[:, t:t + 1].bitcast(F32), None, ALU.is_equal)
                        dve.drain()
                        nc.vector.tensor_tensor_scan(cum, eq, eq, last, ALU.add, ALU.bypass)
                        dve.drain()
                        nc.vector.tensor_copy(last, cum[:, S - 1:S])
                        nc.vector.scalar_tensor_tensor(keep, cum, quota[:, t:t + 1], eq, ALU.is_le, ALU.mult)
                        dve.drain()
                        nc.vector.scalar_tensor_tensor(m, keep, 0.0, m, ALU.is_equal, ALU.mult)
                        dve.drain()

            def search(g):
                search_sums(g, range(TT))
                search_start()
                for _ in range(STEPS):
                    count_below(at)
                    search_move()
                search_pick(range(TT))
                search_end()

            def add_blocks(blocks, p_first, n, y_before):
                for b in range(n):
                    dve.wait_ge(block_done, blocks + b + 1)
                    dst = acc[:, b, :]
                    if p_first:
                        need(dve, y_tr, y_before)
                        ins = nc.vector.tensor_copy(dst, bank_d[b % 2][:, :])
                    else:
                        dve.wait_ge(acc_done, blocks + b - KB + 1)
                        ins = nc.vector.tensor_tensor(dst, dst, bank_d[b % 2][:, :], ALU.add)
                    ins.then_inc(acc_done, 1)

            def phase_u(g):
                c0, pb, bb, hb = g * NC, prods_u(g), blocks_u(g), chunks_u(g)

                def mask(c, r):
                    for t in range(TT):
                        m = mag[:, t, bass.ds(c * P, P)]
                        ins = nc.vector.scalar_tensor_tensor(act_s[:, r, t * P:(t + 1) * P], m,
                                                             kth[:, t:t + 1].bitcast(F32), m,
                                                             ALU.is_ge, ALU.mult)
                    ins.then_inc(masked, 1)

                def ups(p, masks=True):
                    for r in range(2):
                        c = 2 * p + r
                        dve.wait_ge(mask_tr, c0 + c + 1)
                        need(dve, h_done, hb + c)
                        nc.vector.scalar_tensor_tensor(sm[:, :], sign[:, c, :], 0.5,
                                                       bank_t[:, :], ALU.subtract, ALU.mult).then_inc(sm_done, 1)
                        dve.wait_ge(sm_done, c0 + c + 1)
                        dve.wait_ge(job_done, pb + c + 1)
                        need(dve, h_lo_done, hb + c - 1)
                        nc.vector.scalar_tensor_tensor(hf[:, r, :], sm[:, :], 2.0, bank_a[r][:, :],
                                                       ALU.mult, ALU.mult).then_inc(h_done, 1)
                        if masks:
                            mask(c + 2, r)

                mask(0, 0)
                mask(1, 1)
                ups(0)
                ups(1)
                add_blocks(bb, True, 2 * 4, 4 * TT * g)
                with dve.Fori(2, NP - 1) as p:
                    ups(p)
                    add_blocks(bb + 8 * p - 8, False, 8, 0)
                ups(NP - 1, False)
                add_blocks(bb + 8 * NP - 16, False, 8, 0)
                add_blocks(bb + 8 * NP - 8, False, 8, 0)

            def lora_low(dst, n):
                dve.wait_ge(low_hi, n + 1)
                nc.vector.scalar_tensor_tensor(dst[64:P, :], bank_l[64:P, :], LORA_SCALE,
                                               dst[64:P, :].bitcast(F32), ALU.mult,
                                               ALU.subtract).then_inc(low_lo, 1)

            def phase_b(g, last):
                pb, bb, hb = prods_b(g, last), blocks_b(g), chunks_b(g)
                n0 = g * NC
                lora_low(lora_in, 2 * g)

                def product(p, r):
                    c = 2 * p + r
                    dve.wait_ge(ffn_silu, n0 + c + 1)
                    dve.wait_ge(job_done, pb + 2 * c + 3)
                    need(dve, h_lo_done, hb + c - 1)
                    nc.vector.tensor_tensor(hf[:, r, :], act_s[:, r, :], bank_c[r][:, :],
                                            ALU.mult).then_inc(h_done, 1)

                def pairs(p, beside_0=None, beside_1=None, after=None):
                    if not last and beside_0 is not None:
                        beside_0()
                    product(p, 0)
                    if not last and beside_1 is not None:
                        beside_1()
                    product(p, 1)
                    if not last and after is not None:
                        after()

                def step(p):
                    pairs(p, lambda: count_below(at, (0, 1)), lambda: (count_below(at, (2, 3)), search_move()))

                pairs(0, lambda: search_sums(g + 1, (0, 1)), lambda: (search_sums(g + 1, (2, 3)), search_start()))
                step(1)
                add_blocks(bb, True, 8, 4 * TT * g + 2 * TT)
                with dve.Fori(2, STEPS + 1) as p:
                    step(p)
                    add_blocks(bb + 8 * p - 8, False, 8, 0)
                pairs(NP - 2, lambda: search_pick((0,)), lambda: search_pick((1,)))
                add_blocks(bb + 8 * NP - 24, False, 8, 0)
                pairs(NP - 1, lambda: search_pick((2,)), lambda: search_pick((3,)), search_end)
                add_blocks(bb + 8 * NP - 16, False, 8, 0)
                add_blocks(bb + 8 * NP - 8, False, 8, 0)
                lora_low(lora_mid, 2 * g + 1)
                add_blocks(bb + 8 * NP, False, 8, 0)

            for i in range(8):
                nc.vector.memset(rank[:, i:i + 1], float(i + 1))
            nc.vector.memset(bad[:, :], 0.0)
            prepare_a(0)
            phase_g(0)
            search(0)
            phase_u(0)
            finish_a(0)
            with dve.Fori(1, NG) as g:
                prepare_a(g)
                phase_g(g)
                phase_b(g - 1, False)
                finish_b(g - 1, False)
                phase_u(g)
                finish_a(g)
            phase_b(NG - 1, True)
            finish_b(NG - 1, True)


def kernel(**inputs):
    import numpy as np
    import concourse.bacc as bacc
    from concourse.bass_utils import run_bass_kernel_spmd

    a = {k: np.ascontiguousarray(v) for k, v in inputs.items()}
    x = a["L0_attn_x"]
    pad = NC * P - I

    def in_tiles(w, lora=None, rows=()):
        w = np.pad(w, ((0, pad), (0, 0))).reshape(NC, P, KB, P).transpose(0, 3, 2, 1).reshape(NC, P, H)
        if lora is None:
            return np.ascontiguousarray(w)
        b = np.zeros((NC, P, P), w.dtype)
        t = np.pad(lora, ((0, pad), (0, 0))).reshape(NC, P, R).transpose(0, 2, 1)
        for at in rows:
            b[:, at:at + R] = t
        return np.concatenate([w, b], 2)

    def down_tiles(w, lora=None):
        w = np.pad(w, ((0, 0), (0, pad))).reshape(2, 512, NP, 2, P).transpose(2, 0, 4, 3, 1).reshape(NC, P, H)
        if lora is None:
            return np.ascontiguousarray(w)
        b = np.zeros((NC, P, P), w.dtype)
        t = np.pad(lora, ((0, 0), (0, pad))).reshape(R, NC, P).transpose(1, 2, 0)
        for at in (0, 64):
            b[:, :, at:at + R] = t
        return np.concatenate([w, b], 2)

    a13 = np.zeros((P, KB, P), x.dtype)
    for at, name in ((0, "L0_ffn_lora_A1"), (32, "L0_ffn_lora_A3"), (64, "L0_ffn_lora_A1"),
                     (96, "L0_ffn_lora_A3")):
        a13[:, :, at:at + R] = a[name].reshape(R, KB, P).transpose(2, 1, 0)
    a13 = np.concatenate([a13.reshape(P, H), np.zeros((P, P), x.dtype)], 1)
    b2 = np.zeros((P, WX), x.dtype)
    for at in (0, 64):
        b2[at:at + R, 0:H] = a["L0_ffn_lora_B2"].T

    arrays = {
        "x": x.reshape(TOKENS, H),
        "w_gate": in_tiles(a["L0_attn_w_gate"]),
        "w_up": in_tiles(a["L0_attn_w_up"]),
        "w_down": down_tiles(a["L0_attn_w_down"]),
        "w1": in_tiles(a["L0_ffn_w1"], a["L0_ffn_lora_B1"], (0, 64)),
        "w3": in_tiles(a["L0_ffn_w3"], a["L0_ffn_lora_B3"], (32, 96)),
        "w2": down_tiles(a["L0_ffn_w2"], a["L0_ffn_lora_A2"]),
        "lora_a13": a13,
        "lora_b2": b2,
    }
    nc = bacc.Bacc("TRN2", target_bir_lowering=False, num_devices=1)
    ins = {k: nc.dram_tensor(k, v.shape, mybir.dt.from_np(v.dtype), kind="ExternalInput").ap()
           for k, v in arrays.items()}
    out = nc.dram_tensor("out", (TOKENS, H), F32, kind="ExternalOutput").ap()
    ffn_sandwich(nc, **ins, out=out)
    r = run_bass_kernel_spmd(nc, [arrays], core_ids=[0])
    return r.results[0]["out"].reshape(x.shape)
```

```python
from contextlib import ExitStack

import concourse.bass as bass
from concourse import mybir
from concourse.alu_op_type import AluOpType as ALU

F32 = mybir.dt.float32
F32R = mybir.dt.float32r
U32 = mybir.dt.uint32
U8 = mybir.dt.uint8
ACT = mybir.ActivationFunctionType
AX_X = mybir.AxisListType.X

P = 128
TOKENS = 2048
H = 1024
I = 2752
R = 16
KB = H // P
NC = -(-I // P)
NP = NC // 2
NG = 4
TG = TOKENS // NG
TT = TG // P
K_ZERO = I // 2
EPS = 1e-5
Q = I // 4
GUESS = 0.75
STEPS = 7
AIM = 3.5
LORA_SCALE = 2.0
WT = H
WX = H + P

JG = NC
JU = NC + 2 * NP
JB = 1 + 2 * NC + 2 * NP + 1
JC = JG + JU + JB


def need(eng, sem, value):
    if isinstance(value, int) and value <= 0:
        return
    eng.wait_ge(sem, value)


def jobs_g(g):
    return 0 if isinstance(g, int) and g == 0 else g * JC - JB


def jobs_u(g):
    return g * JC + JG


def jobs_b(g, last):
    return g * JC + 2 * JG + JU - (JG if last else 0)


def prods_g(g):
    return 0 if isinstance(g, int) and g == 0 else g * (4 * NC + 1) - 2 * NC - 1


def prods_u(g):
    return g * (4 * NC + 1) + NC


def prods_b(g, last):
    return g * (4 * NC + 1) + (2 if last else 3) * NC


def blocks_u(g):
    return g * (16 * NP + KB)


def blocks_b(g):
    return g * (16 * NP + KB) + 8 * NP


def tiles_ya(g):
    return 2 * TT * g


def tiles_yb(g):
    return 2 * TT * g + TT


def tiles_xa(g):
    return 0 if isinstance(g, int) and g == 0 else TT * (2 * g - 1)


def tiles_xb(g):
    return TT * (2 * g + 2)


def rows_stats(g):
    return 4 * g - 3


def rows_norm(g):
    return 0 if isinstance(g, int) and g == 0 else 4 * g - 2


def rows_mid(g):
    return 4 * g + 3


def rows_out(g):
    return 4 * g + 4


def chunks_u(g):
    return g * 2 * NC


def chunks_b(g):
    return g * 2 * NC + NC


def ffn_sandwich(nc, x, w_gate, w_up, w_down, w1, w3, w2, lora_a13, lora_b2, out):
    ctx = ExitStack()
    with ctx:
        def sb(name, shape, dt):
            return ctx.enter_context(nc.sbuf_tensor(name, shape, dt))

        def bank(name):
            return ctx.enter_context(nc.psum_tensor(name, [P, 512], F32))

        def sem(name):
            return ctx.enter_context(nc.semaphore(name))

        x_mid = nc.dram_tensor("x_mid", (TOKENS // P, P, H), F32, kind="Internal").ap()

        mag = sb("mag", [P, TT, NC * P], F32)
        sign = sb("sign", [P, NC, TG], U8)
        xa_hi = sb("xa_hi", [P, KB, TG], F32R)
        xa_lo = sb("xa_lo", [P, KB, TG], F32R)
        with nc.sbuf_tensor("y_rows", [P, TT * H], F32) as y_rows:
            pass
        xb_hi = sb("xb_hi", [P, KB, TG], F32R)
        xb_lo = sb("xb_lo", [P, KB, TG], F32R)
        acc = sb("acc", [P, KB, TG], F32)
        h_hi = sb("h_hi", [P, 2, 2, TG], F32R)
        h_lo = sb("h_lo", [P, 2, 2, TG], F32R)
        raw = [sb(f"raw{i}", [P, WX], F32) for i in range(2)]
        w_hi = [sb(f"w_hi{i}", [P, WX], F32R) for i in range(2)]
        w_lo = [sb(f"w_lo{i}", [P, WX], F32R) for i in range(2)]
        hf = sb("hf", [P, 2, TG], F32)
        sm = sb("sm", [P, TG], F32)
        act_s = sb("act_s", [P, 2, TG], F32)
        row_y = [sb(f"row_y{i}", [P, H], F32) for i in range(2)]
        row_x = [sb(f"row_x{i}", [P, H], F32) for i in range(2)]
        lora_act = sb("lora_act", [P, TG], F32R)
        ident = sb("ident", [P, P], F32)
        stats = sb("stats", [P, 2, 6], F32)
        mv = sb("mv", [P, 2], F32)
        small = sb("small", [P, 4 * TT], F32)
        ra, rb, rc, bad_q = [small[:, i:i + 1] for i in range(4)]
        next_rs, next_a, next_c = [small[:, (i + 1) * TT:(i + 2) * TT] for i in range(3)]
        next_mv = sb("next_mv", [P, TT, 2], F32)
        cand = sb("cand", [P, TT], U32)
        kth = sb("kth", [P, TT], U32)
        bit = sb("bit", [P, TT], U32)
        below = sb("below", [P, TT], U32)
        cnt = sb("cnt", [P, TT], F32)
        quota = sb("quota", [P, TT], F32)
        at = sb("at", [P, TT], F32)
        at_old = sb("at_old", [P, TT], F32)
        cnt_old = sb("cnt_old", [P, TT], F32)
        best = sb("best", [P, TT], F32)
        best_cnt = sb("best_cnt", [P, TT], F32)
        d_at = sb("d_at", [P, TT], F32)
        d_cnt = sb("d_cnt", [P, TT], F32)
        alt = sb("alt", [P, TT], F32)
        less = sb("less", [P, TT], F32)
        flag = sb("flag", [P, TT], U32)
        tops = sb("tops", [P, 4 * 8], F32)
        top8 = sb("top8", [P, 8], F32)
        picked = sb("picked", [P, 8], F32)
        nxt = sb("nxt", [P, TT], F32)
        rank = sb("rank", [P, 8], F32)
        bad = sb("bad", [P, 32], F32)
        bad_i = sb("bad_i", [P, 1], U32)

        bank_a = [bank("bank_a0"), bank("bank_a1")]
        bank_c = [bank("bank_c0"), bank("bank_c1")]
        bank_d = [bank("bank_d0"), bank("bank_d1")]
        bank_t = bank("bank_t")
        bank_l = bank("bank_l")

        ident_ok = sem("ident_ok")
        lora_clear = sem("lora_clear")
        raw_in = [sem("raw_in0"), sem("raw_in1")]
        hi_done = sem("hi_done")
        lo_done = sem("lo_done")
        job_done = sem("job_done")
        gate_silu = sem("gate_silu")
        gate_sign = sem("gate_sign")
        gate_tr = sem("gate_tr")
        mag_done = sem("mag_done")
        masked = sem("masked")
        mask_tr = sem("mask_tr")
        sm_done = sem("sm_done")
        ffn_silu = sem("ffn_silu")
        h_done = sem("h_done")
        h_hi_done = sem("h_hi_done")
        h_lo_done = sem("h_lo_done")
        block_done = sem("block_done")
        acc_done = sem("acc_done")
        low_hi = sem("low_hi")
        low_lo = sem("low_lo")
        y_tr = sem("y_tr")
        y_copied = sem("y_copied")
        row_in = [sem("row_in0"), sem("row_in1")]
        row_free = sem("row_free")
        mid_ready = sem("mid_ready")
        row_stored = [sem("row_stored0"), sem("row_stored1")]
        out_ready = sem("out_ready")
        xn_done = sem("xn_done")
        xn_tr = sem("xn_tr")
        xt_hi = sem("xt_hi")
        xt_lo = sem("xt_lo")

        x_t = x.rearrange("(n p) h -> n p h", p=P)
        out_t = out.rearrange("(n p) h -> n p h", p=P)

        block = ctx.enter_context(nc.Block())

        @block.sync
        def _(sp):
            def tile(j, r, src, n):
                need(sp, lo_done, j - 1)
                sp.dma_start(raw[r][:, 0:n], src).then_inc(raw_in[r], 16)

            def phase_g(g):
                jb = jobs_g(g)
                for r in range(2):
                    tile(jb + r, r, w_gate[r], WT)
                with sp.Fori(1, NP) as q:
                    for r in range(2):
                        tile(jb + 2 * q + r, r, w_gate[2 * q + r], WT)

            def phase_u(g):
                jb = jobs_u(g)
                for r in range(2):
                    tile(jb + r, r, w_up[r], WT)
                with sp.Fori(1, NP) as p:
                    for r in range(2):
                        tile(jb + 4 * p - 2 + r, r, w_up[2 * p + r], WT)
                    for r in range(2):
                        tile(jb + 4 * p + r, r, w_down[2 * p - 2 + r], WT)
                for r in range(2):
                    tile(jb + JU - 2 + r, r, w_down[2 * NP - 2 + r], WT)

            def phase_b(g, last):
                jb = jobs_b(g, last)
                tile(jb, 0, lora_a13, WX)
                for c in range(2):
                    tile(jb + 1 + 2 * c, 1, w1[c], WX)
                    tile(jb + 2 + 2 * c, 0, w3[c], WX)
                with sp.Fori(1, NP) as p:
                    for c in range(2):
                        tile(jb + 6 * p - 1 + 2 * c, 1, w1[2 * p + c], WX)
                        tile(jb + 6 * p + 2 * c, 0, w3[2 * p + c], WX)
                    for j in range(2):
                        tile(jb + 6 * p + 3 + j, 1 - j, w2[2 * p - 2 + j], WX)
                for j in range(2):
                    tile(jb + JB - 3 + j, 1 - j, w2[2 * NP - 2 + j], WX)
                tile(jb + JB - 1, 1, lora_b2, WX)

            phase_g(0)
            phase_u(0)
            with sp.Fori(1, NG) as g:
                phase_g(g)
                phase_b(g - 1, False)
                phase_u(g)
            phase_b(NG - 1, True)

        @block.tensor
        def _(pe):
            def split_product(dst, r, at, hi, lo, first, last):
                wh, wl = w_hi[r][:, at:at + P], w_lo[r][:, at:at + P]
                nc.tensor.matmul(dst, wh, hi, start=first, stop=False)
                nc.tensor.matmul(dst, wh, lo, start=False, stop=False)
                return nc.tensor.matmul(dst, wl, hi, start=False, stop=last)

            def job_in(dst, j, r, xh, xl, lora=False, lora_ready=0):
                pe.wait_ge(lo_done, j + 1)
                for k in range(KB):
                    ins = split_product(dst, r, k * P, xh[:, k, :], xl[:, k, :], k == 0,
                                        k == KB - 1 and not lora)
                if lora:
                    need(pe, low_lo, lora_ready)
                    nc.tensor.matmul(dst, w_hi[r][:, H:WX], lora_act[:, :], start=False, stop=False)
                    ins = nc.tensor.matmul(dst, w_lo[r][:, H:WX], lora_act[:, :], start=False, stop=True)
                ins.then_inc(job_done, 1)

            def gate_transposes(n, r):
                pe.wait_ge(gate_silu, n + 1)
                need(pe, mag_done, n)
                for t in range(TT):
                    ins = nc.tensor.transpose(bank_t[:, t * P:(t + 1) * P],
                                              act_s[:, r, t * P:(t + 1) * P], ident[:, :])
                ins.then_inc(gate_tr, 1)

            def phase_g(g):
                jb = jobs_g(g)
                n0 = g * NC

                def chunk(c, r, first):
                    if not first:
                        pe.wait_ge(gate_silu, n0 + c - 1)
                    job_in(bank_a[r][:, :], jb + c, r, xa_hi, xa_lo)

                pe.wait_ge(xt_lo, 2 * (tiles_xa(g) + TT))
                chunk(0, 0, True)
                chunk(1, 1, True)
                gate_transposes(n0, 0)
                if not (isinstance(g, int) and g == 0):
                    for q in range(1, NP):
                        t = (q - 1) // 2
                        if q % 2 and t < TT:
                            y_transposes(tiles_ya(g - 1), t, blocks_u(g - 1) + 8 * NP)
                        chunk(2 * q, 0, False)
                        gate_transposes(n0 + 2 * q - 1, 1)
                        if q % 2 and 1 <= t <= TT:
                            xn_transposes(tiles_xb(g - 1), t - 1)
                        chunk(2 * q + 1, 1, False)
                        gate_transposes(n0 + 2 * q, 0)
                    gate_transposes(n0 + NC - 1, 1)
                    return
                with pe.Fori(1, NP) as q:
                    chunk(2 * q, 0, False)
                    gate_transposes(n0 + 2 * q - 1, 1)
                    chunk(2 * q + 1, 1, False)
                    gate_transposes(n0 + 2 * q, 0)
                gate_transposes(n0 + NC - 1, 1)

            def down_job(blocks, j, r, half, slot, p_first, y_before, lora=None):
                pe.wait_ge(lo_done, j + 1)
                if lora is not None:
                    split_product(bank_l[:, :], r, H, h_hi[:, slot, half, :], h_lo[:, slot, half, :], *lora)
                for b in range(4):
                    if p_first and half == 0 and b < 2:
                        need(pe, y_copied, y_before)
                    else:
                        pe.wait_ge(acc_done, blocks + 4 * half + b - 1)
                    for c in range(2):
                        ins = split_product(bank_d[b % 2][:, :], r, c * 512 + b * P, h_hi[:, slot, c, :],
                                            h_lo[:, slot, c, :], c == 0, c == 1)
                    ins.then_inc(block_done, 1)

            def phase_u(g):
                jb, c0, bb = jobs_u(g), g * NC, blocks_u(g)
                hb = chunks_u(g)

                def ups(p, j, first, rows=False):
                    for r in range(2):
                        c = 2 * p + r
                        pe.wait_ge(masked, c0 + c + 1)
                        need(pe, sm_done, c0 + c)
                        for t in range(TT):
                            ins = nc.tensor.transpose(bank_t[:, t * P:(t + 1) * P],
                                                      act_s[:, r, t * P:(t + 1) * P], ident[:, :])
                        ins.then_inc(mask_tr, 1)
                        if not first:
                            pe.wait_ge(h_done, hb + c - 1)
                        job_in(bank_a[r][:, :], j + r, r, xa_hi, xa_lo)
                        if rows:
                            y_transposes(tiles_yb(g - 1), c, blocks_b(g - 1) + 8 * NP + KB)

                def downs(p, j, slot, p_first, xn=None):
                    pe.wait_ge(h_lo_done, hb + 2 * p + 2)
                    for half in range(2):
                        if xn is not None:
                            xn_transposes(tiles_xa(g + 1), xn + half)
                        down_job(bb + 8 * p, j + half, half, half, slot, p_first, 4 * TT * g)

                pe.wait_ge(gate_silu, (g + 1) * NC)
                if not (isinstance(g, int) and g == 0):
                    pe.wait_ge(ffn_silu, g * NC)
                later = not (isinstance(g, int) and g == 0)
                ups(0, jb, True, later)
                ups(1, jb + 2, False, later)
                downs(0, jb + 4, 0, True)
                with pe.Fori(1, NP // 2) as m:
                    for s in range(2):
                        p = 2 * m + s
                        ups(p, jb + 4 * p - 2, False)
                        downs(p - 1, jb + 4 * p, 1 - s, False)
                ups(NP - 1, jb + 4 * NP - 6, False)
                downs(NP - 2, jb + 4 * NP - 4, 1, False, 0)
                downs(NP - 1, jb + 4 * NP - 2, 0, False, 2)

            def y_transposes(n, t, blocks):
                pe.wait_ge(acc_done, blocks)
                for half in range(2):
                    need(pe, y_copied, 2 * (n + t))
                    for b in range(4):
                        ins = nc.tensor.transpose(bank_d[half][:, b * P:(b + 1) * P],
                                                  acc[:, 4 * half + b, t * P:(t + 1) * P], ident[:, :])
                    ins.then_inc(y_tr, 1)

            def xn_transposes(n, t):
                pe.wait_ge(xn_done, n + t + 1)
                need(pe, xt_lo, 2 * (n + t))
                for half in range(2):
                    for b in range(4):
                        k = 4 * half + b
                        ins = nc.tensor.transpose(bank_c[half][:, b * P:(b + 1) * P],
                                                  row_y[t % 2][:, k * P:(k + 1) * P], ident[:, :])
                    ins.then_inc(xn_tr, 1)

            def phase_b(g, last):
                jb, bb, hb = jobs_b(g, last), blocks_b(g), chunks_b(g)
                n0 = g * NC
                pe.wait_ge(xt_lo, 2 * (tiles_xb(g) + TT))
                pe.wait_ge(gate_silu, (g + 1 if last else g + 2) * NC)
                pe.wait_ge(lo_done, jb + 1)
                need(pe, low_lo, 2 * g)
                for k in range(KB):
                    ins = split_product(bank_l[:, :], 0, k * P, xb_hi[:, k, :], xb_lo[:, k, :],
                                        k == 0, k == KB - 1)
                ins.then_inc(job_done, 1)

                def pairs(p, j, first):
                    for c in range(2):
                        if not first:
                            pe.wait_ge(ffn_silu, n0 + 2 * p + c - 1)
                        job_in(bank_a[c][:, :], j + 2 * c, 1, xb_hi, xb_lo, True, 2 * g + 1 if first else 0)
                        if not first:
                            pe.wait_ge(h_done, hb + 2 * p + c - 1)
                        job_in(bank_c[c][:, :], j + 2 * c + 1, 0, xb_hi, xb_lo, True)

                def downs(p, j, slot, p_first, p_last=False):
                    pe.wait_ge(h_lo_done, hb + 2 * p + 2)
                    for half in range(2):
                        down_job(bb + 8 * p, j + half, 1 - half, half, slot, p_first,
                                 4 * TT * g + 2 * TT, (p_first and half == 0, p_last and half == 1))

                pairs(0, jb + 1, True)
                pairs(1, jb + 5, False)
                downs(0, jb + 9, 0, True)
                with pe.Fori(1, NP // 2) as m:
                    for s in range(2):
                        p = 2 * m + s
                        pairs(p, jb + 6 * p - 1, False)
                        downs(p - 1, jb + 6 * p + 3, 1 - s, False)
                pairs(NP - 1, jb + 6 * NP - 7, False)
                downs(NP - 2, jb + 6 * NP - 3, 1, False)
                downs(NP - 1, jb + JB - 3, 0, False, True)
                pe.wait_ge(low_lo, 2 * g + 2)
                pe.wait_ge(lo_done, jb + JB)
                for b in range(KB):
                    pe.wait_ge(acc_done, bb + 8 * NP + b - 1)
                    nc.tensor.matmul(bank_d[b % 2][:, :], w_hi[1][:, b * P:(b + 1) * P], lora_act[:, :],
                                     start=True, stop=False)
                    ins = nc.tensor.matmul(bank_d[b % 2][:, :], w_lo[1][:, b * P:(b + 1) * P],
                                           lora_act[:, :], start=False, stop=True)
                    ins.then_inc(block_done, 1)

            pe.wait_ge(ident_ok, 2)
            for t in range(TT):
                xn_transposes(0, t)
            phase_g(0)
            phase_u(0)
            with pe.Fori(1, NG) as g:
                phase_g(g)
                phase_b(g - 1, False)
                phase_u(g)
            for t in range(TT):
                y_transposes(tiles_ya(NG - 1), t, blocks_u(NG - 1) + 8 * NP)
                if t:
                    xn_transposes(tiles_xb(NG - 1), t - 1)
            xn_transposes(tiles_xb(NG - 1), TT - 1)
            phase_b(NG - 1, True)
            for t in range(TT):
                y_transposes(tiles_yb(NG - 1), t, blocks_b(NG - 1) + 8 * NP + KB)

        @block.scalar
        def _(act):
            def w_high(j, r, n, free, value):
                need(act, free, value)
                act.wait_ge(raw_in[r], 8 * (j - r) + 16)
                nc.scalar.activation(w_hi[r][:, 0:n], raw[r][:, 0:n], ACT.Copy).then_inc(hi_done, 1)

            def h_high(n, slot, r):
                act.wait_ge(h_done, n + 1)
                nc.scalar.activation(h_hi[:, slot, r, :], hf[:, r, :], ACT.Copy).then_inc(h_hi_done, 1)

            def phase_g(g, width):
                jb, n0, pb = jobs_g(g), g * NC, prods_g(g)

                def chunk(c, r, n, first):
                    w_high(jb + c + 2, r, n, job_done, pb + c + 1)
                    if first:
                        need(act, h_done, 0 if isinstance(g, int) and g == 0 else g * 2 * NC - NC)
                    else:
                        act.wait_ge(gate_tr, n0 + c - 1)
                        act.wait_ge(gate_sign, n0 + c - 1)
                    nc.scalar.activation(act_s[:, r, :], bank_a[r][:, :], ACT.Silu).then_inc(gate_silu, 1)

                def magnitude(c):
                    act.wait_ge(gate_tr, n0 + c + 1)
                    nc.scalar.activation(mag[:, :, bass.ds(c * P, P)],
                                         bank_t[:, :].rearrange("p (t i) -> p t i", t=TT),
                                         ACT.Abs).then_inc(mag_done, 1)

                chunk(0, 0, WT, True)
                chunk(1, 1, WT, True)
                magnitude(0)
                if not (isinstance(g, int) and g == 0):
                    load_mid(g - 1, 0)
                    load_mid(g - 1, 1)
                    for q in range(1, NP - 1):
                        t = (q - 1) // 2
                        chunk(2 * q, 0, WT, False)
                        magnitude(2 * q - 1)
                        if q % 2 and t < TT:
                            y_copy_a(g - 1, t)
                        elif t < TT:
                            store_mid(g - 1, t)
                        chunk(2 * q + 1, 1, WT, False)
                        magnitude(2 * q)
                        if q % 2 and 1 <= t <= TT:
                            x_high(xb_hi, tiles_xb(g - 1), t - 1)
                            if t + 1 < TT:
                                load_mid(g - 1, t + 1)
                    chunk(NC - 2, 0, width, False)
                    magnitude(NC - 3)
                    chunk(NC - 1, 1, width, False)
                    magnitude(NC - 2)
                    magnitude(NC - 1)
                    return
                with act.Fori(1, NP - 1) as q:
                    chunk(2 * q, 0, WT, False)
                    magnitude(2 * q - 1)
                    chunk(2 * q + 1, 1, WT, False)
                    magnitude(2 * q)
                chunk(NC - 2, 0, width, False)
                magnitude(NC - 3)
                chunk(NC - 1, 1, width, False)
                magnitude(NC - 2)
                magnitude(NC - 1)

            def phase_u(g):
                jb, pb, bb, hb = jobs_u(g), prods_u(g), blocks_u(g), chunks_u(g)

                later = not (isinstance(g, int) and g == 0)

                def ups(p, j, slot, rows=False):
                    for r in range(2):
                        w_high(j + r + 2, r, WT, job_done, pb + 2 * p + r + 1)
                        h_high(hb + 2 * p + r, slot, r)
                        if rows:
                            y_copy_b(g - 1, 2 * p + r)

                def downs(p, j, n, xn=None):
                    for half in range(2):
                        if xn is not None:
                            t = xn + half
                            x_high(xa_hi, tiles_xa(g + 1), t)
                            if t in (0, 1):
                                load(rows_norm(g + 1), t + 2, x_t[TT * g + TT + t + 2])
                        w_high(j + half + 2, half, n, block_done, bb + 8 * p + 4 * half + 4)

                ups(0, jb, 0, later)
                ups(1, jb + 2, 1, later)
                downs(0, jb + 4, WT)
                with act.Fori(1, 3) as m:
                    for s in range(2):
                        p = 2 * m + s
                        if later:
                            t = 2 * m - 2 + s
                            act.wait_ge(row_free, TT * rows_out(g - 1) + t - 1)
                            act.wait_ge(row_stored[s], 16 * (4 * g - 3 + m))
                            act.dma_start(row_x[s][:, :], x_mid[TT * g - TT + t]).then_inc(row_in[s], 16)
                        ups(p, jb + 4 * p - 2, s)
                        if later:
                            act.wait_ge(out_ready, TT * g - TT + t + 1)
                            act.dma_start(out_t[TT * g - TT + t], row_x[s][:, :]).then_inc(row_stored[s], 16)
                        downs(p - 1, jb + 4 * p, WT)
                with act.Fori(3, 5) as m:
                    for s in range(2):
                        p = 2 * m + s
                        t = 2 * m - 6 + s
                        act.wait_ge(row_free, TT * rows_stats(g + 1) + t - 1)
                        if later:
                            act.wait_ge(row_stored[s], 64 * g)
                        act.dma_start(row_x[s][:, :], x_t[TT * g + TT + t]).then_inc(row_in[s], 16)
                        ups(p, jb + 4 * p - 2, s)
                        downs(p - 1, jb + 4 * p, WT)
                for t in range(2):
                    load(rows_norm(g + 1), t, x_t[TT * g + TT + t])
                ups(NP - 1, jb + 4 * NP - 6, 0)
                downs(NP - 2, jb + 4 * NP - 4, WT, 0)
                downs(NP - 1, jb + 4 * NP - 2, WX, 2)

            def phase_b(g, last):
                jb, pb, bb, hb = jobs_b(g, last), prods_b(g, last), blocks_b(g), chunks_b(g)
                n0 = g * NC
                w_high(jb + 2, 0, WX, job_done, pb + 1)
                nc.scalar.activation(lora_act[:, :], bank_l[:, :], ACT.Copy, scale=LORA_SCALE).then_inc(low_hi, 1)

                def pairs(p, j, slot, first):
                    for c in range(2):
                        k = 2 * p + c
                        w_high(j + 2 * c + 2, 1, WX, job_done, pb + 2 * k + 2)
                        if first:
                            act.wait_ge(gate_sign, (g + 1 if last else g + 2) * NC)
                        else:
                            act.wait_ge(h_done, hb + k - 1)
                        nc.scalar.activation(act_s[:, c, :], bank_a[c][:, :], ACT.Silu).then_inc(ffn_silu, 1)
                        w_high(j + 2 * c + 3, 0, WX, job_done, pb + 2 * k + 3)
                        h_high(hb + k, slot, c)

                def downs(p, j, n):
                    for half in range(2):
                        w_high(j + half + 2, 1 - half, WX, block_done, bb + 8 * p + 4 * half + 4)

                pairs(0, jb + 1, 0, True)
                pairs(1, jb + 5, 1, False)
                downs(0, jb + 9, WX)
                with act.Fori(1, NP // 2) as m:
                    for s in range(2):
                        p = 2 * m + s
                        pairs(p, jb + 6 * p - 1, s, False)
                        downs(p - 1, jb + 6 * p + 3, WX)
                pairs(NP - 1, jb + 6 * NP - 7, 0, False)
                downs(NP - 2, jb + 6 * NP - 3, WX)
                w_high(jb + JB - 1, 1, WX, block_done, bb + 8 * NP - 4)
                if not last:
                    w_high(jb + JB, 0, WT, block_done, bb + 8 * NP)
                act.wait_ge(block_done, bb + 8 * NP)
                nc.scalar.activation(lora_act[:, :], bank_l[:, :], ACT.Copy, scale=LORA_SCALE).then_inc(low_hi, 1)
                if not last:
                    w_high(jb + JB + 1, 1, WT, block_done, bb + 8 * NP + KB)

            def load(k, t, src):
                need(act, row_free, TT * k + t - 1)
                act.dma_start(row_x[t % 2][:, :], src).then_inc(row_in[t % 2], 16)

            def load_mid(g, t):
                if t >= 2:
                    act.wait_ge(row_stored[t % 2], 16 * (4 * g + 1))
                load(rows_mid(g), t, x_t[TT * g + t])

            def load_out(g, t):
                act.wait_ge(row_stored[t % 2], 16 * (4 * g + 2 + t // 2))
                load(rows_out(g), t, x_mid[TT * g + t])

            def store_mid(g, t):
                act.wait_ge(mid_ready, TT * g + t + 1)
                act.dma_start(x_mid[TT * g + t], row_x[t % 2][:, :]).then_inc(row_stored[t % 2], 16)

            def store_out(g, t):
                act.wait_ge(out_ready, TT * g + t + 1)
                act.dma_start(out_t[TT * g + t], row_x[t % 2][:, :]).then_inc(row_stored[t % 2], 16)

            def x_high(dst, n, t):
                for half in range(2):
                    act.wait_ge(xn_tr, 2 * (n + t) + half + 1)
                    nc.scalar.activation(dst[:, 4 * half:4 * half + 4, t * P:(t + 1) * P],
                                         bank_c[half][:, :].rearrange("p (k i) -> p k i", k=4),
                                         ACT.Copy).then_inc(xt_hi, 1)

            def y_copy(dst, n, t):
                for half in range(2):
                    act.wait_ge(y_tr, 2 * (n + t) + half + 1)
                    nc.scalar.activation(dst[:, half * 512:half * 512 + 512], bank_d[half][:, :],
                                         ACT.Copy).then_inc(y_copied, 1)

            def y_copy_a(g, t):
                act.wait_ge(xn_tr, 2 * (tiles_xb(g) + t - 1))
                y_copy(row_y[t % 2], tiles_ya(g), t)

            def y_copy_b(g, t):
                y_copy(y_rows[:, t * H:(t + 1) * H], tiles_yb(g), t)

            for t in range(TT):
                load(rows_norm(0), t, x_t[t])
            act.wait_ge(lora_clear, 2)
            for r in range(2):
                w_high(r, r, WT, job_done, 0)
            for t in range(TT):
                x_high(xa_hi, 0, t)
            phase_g(0, WT)
            phase_u(0)
            with act.Fori(1, NG) as g:
                phase_g(g, WX)
                phase_b(g - 1, False)
                phase_u(g)
            g = NG - 1
            load_mid(g, 0)
            load_mid(g, 1)
            for t in range(TT):
                y_copy_a(g, t)
                if t:
                    x_high(xb_hi, tiles_xb(g), t - 1)
                store_mid(g, t)
                if t in (1, 2):
                    load_mid(g, t + 1)
            x_high(xb_hi, tiles_xb(g), TT - 1)
            load_out(g, 0)
            load_out(g, 1)
            phase_b(g, True)
            for t in range(TT):
                y_copy_b(g, t)
                if t:
                    store_out(g, t - 1)
                if t in (1, 2):
                    load_out(g, t + 1)
            store_out(g, TT - 1)
            for s in range(2):
                act.wait_ge(row_stored[s], 16 * TT * NG)

        @block.gpsimd
        def _(pool):
            def w_low(j, r, n):
                pool.wait_ge(hi_done, j + 1)
                nc.gpsimd.tensor_tensor(w_lo[r][:, 0:n], raw[r][:, 0:n], w_hi[r][:, 0:n],
                                        ALU.subtract).then_inc(lo_done, 1)

            def h_low(n, slot, r):
                pool.wait_ge(h_hi_done, n + 1)
                nc.gpsimd.tensor_tensor(h_lo[:, slot, r, :], hf[:, r, :], h_hi[:, slot, r, :],
                                        ALU.subtract).then_inc(h_lo_done, 1)

            def phase_g(g, width):
                jb = jobs_g(g)
                with pool.Fori(0, NP - 1) as q:
                    for r in range(2):
                        w_low(jb + 2 * q + r + 2, r, WT)
                for r in range(2):
                    w_low(jb + NC + r, r, width)

            def phase_u(g):
                jb, hb = jobs_u(g), chunks_u(g)

                def ups(p, j, slot):
                    for r in range(2):
                        w_low(j + r + 2, r, WT)
                        h_low(hb + 2 * p + r, slot, r)

                def downs(j, n):
                    for half in range(2):
                        w_low(j + half + 2, half, n)

                ups(0, jb, 0)
                ups(1, jb + 2, 1)
                downs(jb + 4, WT)
                with pool.Fori(1, NP // 2) as m:
                    for s in range(2):
                        p = 2 * m + s
                        ups(p, jb + 4 * p - 2, s)
                        downs(jb + 4 * p, WT)
                ups(NP - 1, jb + 4 * NP - 6, 0)
                downs(jb + 4 * NP - 4, WT)
                downs(jb + 4 * NP - 2, WX)

            def phase_b(g, last):
                jb, hb = jobs_b(g, last), chunks_b(g)
                w_low(jb + 2, 0, WX)

                def pairs(p, j, slot):
                    for c in range(2):
                        w_low(j + 2 * c + 2, 1, WX)
                        w_low(j + 2 * c + 3, 0, WX)
                        h_low(hb + 2 * p + c, slot, c)

                def downs(j):
                    for half in range(2):
                        w_low(j + half + 2, 1 - half, WX)

                pairs(0, jb + 1, 0)
                pairs(1, jb + 5, 1)
                downs(jb + 9)
                with pool.Fori(1, NP // 2) as m:
                    for s in range(2):
                        p = 2 * m + s
                        pairs(p, jb + 6 * p - 1, s)
                        downs(jb + 6 * p + 3)
                pairs(NP - 1, jb + 6 * NP - 7, 0)
                downs(jb + 6 * NP - 3)
                w_low(jb + JB - 1, 1, WX)
                if not last:
                    w_low(jb + JB, 0, WT)
                    w_low(jb + JB + 1, 1, WT)

            nc.gpsimd.memset(ident[:, :], 0.0).then_inc(ident_ok, 1)
            pool.wait_ge(ident_ok, 1)
            nc.gpsimd.affine_select(out=ident[:, :], in_=ident[:, :], compare_op=ALU.not_equal, fill=1.0,
                                    base=0, pattern=[[-1, P]], channel_multiplier=1).then_inc(ident_ok, 1)
            for r in range(2):
                nc.gpsimd.memset(raw[r][:, WT:WX], 0.0).then_inc(lora_clear, 1)
            for r in range(2):
                w_low(r, r, WT)
            phase_g(0, WT)
            phase_u(0)
            with pool.Fori(1, NG) as g:
                phase_g(g, WX)
                phase_b(g - 1, False)
                phase_u(g)
            phase_b(NG - 1, True)

        @block.vector
        def _(dve):
            def moments(row, to):
                for i in range(2):
                    nc.vector.bn_stats(stats[:, i, :], row[:, i * 512:(i + 1) * 512])
                dve.drain()
                return nc.vector.bn_aggr(to, stats[:, :, :])

            def inverse_root(dst, var, a, c):
                nc.vector.tensor_scalar(a, var, EPS, None, ALU.add)
                dve.drain()
                nc.vector.tensor_scalar(dst.bitcast(mybir.dt.int32), a.bitcast(mybir.dt.int32),
                                        -0.5, float(0x5F3759DF), ALU.mult, ALU.add)
                dve.drain()
                for _ in range(4):
                    nc.vector.scalar_tensor_tensor(c, dst, -0.5, dst, ALU.mult, ALU.mult)
                    dve.drain()
                    nc.vector.tensor_tensor(c, c, a, ALU.mult)
                    dve.drain()
                    nc.vector.scalar_tensor_tensor(dst, c, 1.5, dst, ALU.add, ALU.mult)
                    dve.drain()

            def statistics(row):
                moments(row, mv[:, :])
                dve.drain()
                inverse_root(rb[:, :], mv[:, 1:2], ra[:, :], rc[:, :])

            def normalise(dst, src, mean, inv):
                return nc.vector.tensor_scalar(dst[:, :], src[:, :], mean, inv, ALU.subtract, ALU.mult)

            def x_low(hi, lo, n, t):
                for half in range(2):
                    dve.wait_ge(xt_hi, 2 * (n + t) + half + 1)
                    s = (slice(None), slice(4 * half, 4 * half + 4), slice(t * P, (t + 1) * P))
                    nc.vector.tensor_tensor(lo[s], bank_c[half][:, :].rearrange("p (k i) -> p k i", k=4),
                                            hi[s].bitcast(F32), ALU.subtract).then_inc(xt_lo, 1)

            def rows_here(k, t):
                dve.wait_ge(row_in[t % 2], 16 * (2 * k + t // 2 + 1))

            def rows_to_xn(k, n, t, mean, inv):
                need(dve, xn_tr, 2 * (n + t - 1))
                normalise(row_y[t % 2], row_x[t % 2], mean, inv).then_inc(xn_done, 1)
                dve.drain().then_inc(row_free, 1)

            def mid_rows(g, t):
                y, x = row_y[t % 2], row_x[t % 2]
                dve.wait_ge(y_copied, 2 * (tiles_ya(g) + t + 1))
                statistics(y)
                normalise(y, y, mv[:, 0:1], rb[:, :])
                dve.drain()
                rows_here(rows_mid(g), t)
                nc.vector.tensor_tensor(x[:, :], x[:, :], y[:, :], ALU.add).then_inc(mid_ready, 1)

            def mid_to_xn(g, t):
                dve.drain()
                statistics(row_x[t % 2])
                rows_to_xn(rows_mid(g), tiles_xb(g), t, mv[:, 0:1], rb[:, :])

            def out_statistics(g, t):
                dve.wait_ge(y_copied, 2 * (tiles_yb(g) + t + 1))
                for i in range(2):
                    nc.vector.bn_stats(stats[:, i, :], y_rows[:, bass.ds(t * H + i * 512, 512)])
                dve.drain()
                nc.vector.bn_aggr(mv[:, :], stats[:, :, :])
                dve.drain()
                inverse_root(rb[:, :], mv[:, 1:2], ra[:, :], rc[:, :])

            def out_rows(g, t, s, here):
                y = y_rows[:, bass.ds(t * H, H)]
                nc.vector.tensor_scalar(y, y, mv[:, 0:1], rb[:, :], ALU.subtract, ALU.mult)
                dve.drain()
                dve.wait_ge(row_in[s], here)
                nc.vector.tensor_tensor(row_x[s][:, :], row_x[s][:, :], y, ALU.add).then_inc(out_ready, 1)
                dve.drain().then_inc(row_free, 1)

            def phase_g(g):
                n0 = g * NC

                def signs(c, r):
                    dve.wait_ge(gate_silu, n0 + c + 1)
                    nc.vector.tensor_scalar(sign[:, c, :] if isinstance(c, int) else sign[:, bass.ds(c, 1), :],
                                            act_s[:, r, :] if isinstance(c, int) else act_s[:, r:r + 1, :],
                                            0.0, None, ALU.is_ge).then_inc(gate_sign, 1)

                if not (isinstance(g, int) and g == 0):
                    for q in range(NP):
                        for r in range(2):
                            signs(2 * q + r, r)
                        t = (q - 1) // 2
                        if q % 2 and t < TT:
                            mid_rows(g - 1, t)
                        elif not q % 2 and 0 <= t < TT:
                            mid_to_xn(g - 1, t)
                        if q % 2 and 1 <= t <= TT:
                            x_low(xb_hi, xb_lo, tiles_xb(g - 1), t - 1)
                    return
                with dve.Fori(0, NP) as q:
                    for r in range(2):
                        signs(2 * q + r, r)

            def count_below(bound, tiles=range(TT)):
                junk = [row_y[i][:, :].bitcast(U8)[:, 0:I] for i in range(2)]
                for t in tiles:
                    nc.vector.tensor_scalar(junk[t % 2], mag[:, t, 0:I], bound[:, t:t + 1], None,
                                            ALU.is_lt, ALU.add, accum_out=cnt[:, t:t + 1])
                    if t % 2:
                        dve.drain()

            def search_sums(g, tiles):
                if tiles[0] == 0:
                    dve.wait_ge(mag_done, (g + 1) * NC)
                    dve.wait_ge(xn_tr, 2 * (tiles_xb(g - 1) + TT))
                for t in tiles:
                    for i in range(4):
                        nc.vector.tensor_scalar(row_y[i % 2][:, 0:Q], mag[:, t, i * Q:(i + 1) * Q], 1.0, None,
                                                ALU.mult, ALU.add, accum_out=tops[:, 4 * t + i:4 * t + i + 1])
                        if i % 2:
                            dve.drain()

            def search_start():
                nc.vector.tensor_reduce(at[:, :], tops[:, 0:4 * TT].rearrange("p (t i) -> p t i", i=4), AX_X, ALU.add)
                nc.vector.memset(at_old[:, :], 0.0)
                nc.vector.memset(cnt_old[:, :], 0.0)
                nc.vector.memset(best[:, :], 0.0)
                nc.vector.memset(best_cnt[:, :], 4.0 * I)
                dve.drain()
                nc.vector.tensor_scalar(at[:, :], at[:, :], GUESS / I, None, ALU.mult)
                dve.drain()

            def search_move():
                nc.vector.tensor_tensor(less[:, :], cnt[:, :], best_cnt[:, :], ALU.is_lt)
                nc.vector.tensor_tensor(d_cnt[:, :], cnt[:, :], cnt_old[:, :], ALU.subtract)
                nc.vector.tensor_tensor(d_at[:, :], at[:, :], at_old[:, :], ALU.subtract)
                nc.vector.tensor_scalar(alt[:, :], cnt[:, :], 1.0, None, ALU.add)
                dve.drain()
                nc.vector.scalar_tensor_tensor(flag[:, :], cnt[:, :], float(K_ZERO), less[:, :], ALU.is_ge, ALU.mult)
                nc.vector.tensor_scalar(below[:, :], d_cnt[:, :], 0.0, None, ALU.is_equal)
                dve.drain()
                nc.vector.copy_predicated(best[:, :], flag[:, :], at[:, :])
                nc.vector.copy_predicated(best_cnt[:, :], flag[:, :], cnt[:, :])
                nc.vector.copy_predicated(d_at[:, :], below[:, :], at[:, :])
                nc.vector.copy_predicated(d_cnt[:, :], below[:, :], alt[:, :])
                nc.vector.tensor_scalar(less[:, :], cnt[:, :], -1.0, K_ZERO + AIM, ALU.mult, ALU.add)
                nc.vector.tensor_copy(at_old[:, :], at[:, :])
                nc.vector.tensor_copy(cnt_old[:, :], cnt[:, :])
                dve.drain()
                nc.vector.reciprocal(alt[:, :], d_cnt[:, :])
                nc.vector.tensor_tensor(d_at[:, :], d_at[:, :], less[:, :], ALU.mult)
                dve.drain()
                nc.vector.tensor_tensor(d_at[:, :], d_at[:, :], alt[:, :], ALU.mult)
                dve.drain()
                nc.vector.tensor_tensor(at[:, :], at[:, :], d_at[:, :], ALU.add)
                dve.drain()

            def search_pick(tiles):
                for t in tiles:
                    for i in range(4):
                        part = row_y[i % 2][:, 0:Q]
                        m = mag[:, t, i * Q:(i + 1) * Q]
                        nc.vector.scalar_tensor_tensor(part, m, best[:, t:t + 1], m, ALU.is_lt, ALU.mult)
                        dve.drain()
                        nc.vector.max(tops[:, i * 8:(i + 1) * 8], part)
                    if t == 0:
                        nc.vector.tensor_scalar(less[:, :], best_cnt[:, :], -float(K_ZERO), None, ALU.add)
                        nc.vector.tensor_scalar(alt[:, :], best_cnt[:, :], 1.0 - K_ZERO, None, ALU.add)
                    dve.drain()
                    nc.vector.max(top8[:, :], tops[:, :])
                    dve.drain()
                    nc.vector.scalar_tensor_tensor(picked[:, :], rank[:, :], less[:, t:t + 1], top8[:, :],
                                                   ALU.is_equal, ALU.mult, accum_out=kth[:, t:t + 1].bitcast(F32))
                    dve.drain()
                    nc.vector.scalar_tensor_tensor(picked[:, :], rank[:, :], alt[:, t:t + 1], top8[:, :],
                                                   ALU.is_equal, ALU.mult, accum_out=nxt[:, t:t + 1])
                    dve.drain()

            def search_end():
                nc.vector.tensor_scalar(below[:, :], less[:, :], 0.0, None, ALU.is_equal)
                dve.drain()
                nc.vector.copy_predicated(kth[:, :], below[:, :], best[:, :].bitcast(U32))
                dve.drain()
                nc.vector.tensor_tensor(alt[:, :], nxt[:, :], kth[:, :].bitcast(F32), ALU.is_lt)
                dve.drain()
                nc.vector.scalar_tensor_tensor(alt[:, :], less[:, :], 7.5, alt[:, :], ALU.is_lt, ALU.mult)
                dve.drain()
                nc.vector.tensor_scalar(alt[:, :], alt[:, :], 1.0, None, ALU.is_lt)
                dve.drain()
                nc.vector.tensor_reduce(bad[:, 0:1], alt[:, :], AX_X, ALU.max)
                dve.drain()
                nc.vector.transpose(tops[:, :], bad[:, :])
                dve.drain()
                nc.vector.tensor_reduce(bad_q[:, :], tops[:, :], AX_X, ALU.max)
                dve.drain()
                nc.vector.tensor_copy(bad_i[:, :], bad_q[:, :])
                dve.drain()
                n = [nc.vector.value_load(bad_i[q:q + 1, 0:1], min_val=0, max_val=1) for q in range(0, P, 32)]
                with dve.If(n[0] + n[1] + n[2] + n[3] > 0):
                    search_all()
                dve.drain()

            def search_all():
                nc.vector.memset(kth[:, :], 0)
                nc.vector.memset(bit[:, :], 1 << 30)
                nc.vector.memset(cand[:, :], 1 << 30)
                dve.drain()
                with dve.Fori(0, 31):
                    count_below(cand[:, :].bitcast(F32))
                    nc.vector.tensor_scalar(below[:, :], cnt[:, :], float(K_ZERO), None, ALU.is_lt)
                    dve.drain()
                    nc.vector.copy_predicated(kth[:, :], below[:, :], cand[:, :])
                    nc.vector.tensor_scalar(bit[:, :], bit[:, :], 1, None, ALU.logical_shift_right)
                    dve.drain()
                    nc.vector.tensor_tensor(cand[:, :], kth[:, :], bit[:, :], ALU.bitwise_or)
                    dve.drain()
                count_below(kth[:, :].bitcast(F32))
                nc.vector.tensor_scalar(quota[:, :], cnt[:, :], -1.0, float(K_ZERO), ALU.mult, ALU.add)
                dve.drain()
                S = 344
                eq, cum, keep = row_y[0][:, 0:S], row_y[1][:, 0:S], row_y[1][:, S:2 * S]
                last = row_y[1][:, 2 * S:2 * S + 1]
                for t in range(TT):
                    nc.vector.memset(last, 0.0)
                    dve.drain()
                    with dve.Fori(0, I // S) as i:
                        m = mag[:, t, bass.ds(i * S, S)]
                        nc.vector.tensor_scalar(eq, m, kth[:, t:t + 1].bitcast(F32), None, ALU.is_equal)
                        dve.drain()
                        nc.vector.tensor_tensor_scan(cum, eq, eq, last, ALU.add, ALU.bypass)
                        dve.drain()
                        nc.vector.tensor_copy(last, cum[:, S - 1:S])
                        nc.vector.scalar_tensor_tensor(keep, cum, quota[:, t:t + 1], eq, ALU.is_le, ALU.mult)
                        dve.drain()
                        nc.vector.scalar_tensor_tensor(m, keep, 0.0, m, ALU.is_equal, ALU.mult)
                        dve.drain()

            def search(g):
                search_sums(g, range(TT))
                search_start()
                for _ in range(STEPS):
                    count_below(at)
                    search_move()
                search_pick(range(TT))
                search_end()

            def add_blocks(blocks, p_first, n, y_before, first=0):
                for b in range(first, first + n):
                    dve.wait_ge(block_done, blocks + b + 1)
                    dst = acc[:, b, :]
                    if p_first:
                        need(dve, y_tr, y_before)
                        ins = nc.vector.tensor_copy(dst, bank_d[b % 2][:, :])
                    else:
                        dve.wait_ge(acc_done, blocks + b - KB + 1)
                        ins = nc.vector.tensor_tensor(dst, dst, bank_d[b % 2][:, :], ALU.add)
                    ins.then_inc(acc_done, 1)

            def mask(c, r):
                for t in range(TT):
                    m = mag[:, t, bass.ds(c * P, P)]
                    ins = nc.vector.scalar_tensor_tensor(act_s[:, r, t * P:(t + 1) * P], m,
                                                         kth[:, t:t + 1].bitcast(F32), m,
                                                         ALU.is_ge, ALU.mult)
                ins.then_inc(masked, 1)

            def phase_u(g):
                c0, pb, bb, hb = g * NC, prods_u(g), blocks_u(g), chunks_u(g)

                later = not (isinstance(g, int) and g == 0)

                def up(p, r, beside=None):
                    c = 2 * p + r
                    dve.wait_ge(mask_tr, c0 + c + 1)
                    need(dve, h_done, hb + c)
                    nc.vector.scalar_tensor_tensor(sm[:, :], sign[:, c, :], 0.5,
                                                   bank_t[:, :], ALU.subtract, ALU.mult).then_inc(sm_done, 1)
                    if beside is not None:
                        beside()
                    dve.wait_ge(sm_done, c0 + c + 1)
                    dve.wait_ge(job_done, pb + c + 1)
                    need(dve, h_lo_done, hb + c - 1)
                    nc.vector.scalar_tensor_tensor(hf[:, r, :], sm[:, :], 2.0, bank_a[r][:, :],
                                                   ALU.mult, ALU.mult).then_inc(h_done, 1)

                def stage(p, beside_0=None, beside_1=None):
                    up(p, 0, beside_0)
                    mask(2 * p + 2, 0)
                    up(p, 1, beside_1)
                    add_blocks(bb + 8 * p - 8, False, 4, 0)
                    mask(2 * p + 3, 1)
                    add_blocks(bb + 8 * p - 8, False, 4, 0, 4)

                def next_moments(t, s, here):
                    dve.wait_ge(row_in[s], here)
                    moments(row_x[s], mv[:, :])
                    dve.drain().then_inc(row_free, 1)
                    nc.vector.tensor_copy(next_mv[:, bass.ds(t, 1), :],
                                          mv[:, :].rearrange("p (o c) -> p o c", o=1))

                for p in range(2):
                    for r in range(2):
                        up(p, r)
                        mask(2 * p + r + 2, r)
                add_blocks(bb, True, 8, 4 * TT * g)
                with dve.Fori(1, 3) as m:
                    for s in range(2):
                        t = 2 * m - 2 + s
                        if later:
                            stage(2 * m + s, lambda: out_statistics(g - 1, t),
                                  lambda: out_rows(g - 1, t, s, 16 * (2 * rows_out(g - 1) + m)))
                        else:
                            stage(2 * m + s)
                with dve.Fori(3, 5) as m:
                    for s in range(2):
                        stage(2 * m + s, None, lambda: next_moments(2 * m - 6 + s, s,
                                                                    16 * (2 * rows_stats(g + 1) + m - 2)))

                def next_row(t):
                    rows_here(rows_norm(g + 1), t)
                    rows_to_xn(rows_norm(g + 1), tiles_xa(g + 1), t, next_mv[:, t, 0:1], next_rs[:, t:t + 1])

                def first_row():
                    dve.drain()
                    inverse_root(next_rs[:, :], next_mv[:, :, 1], next_a[:, :], next_c[:, :])
                    next_row(0)

                up(NP - 1, 0, first_row)
                up(NP - 1, 1, lambda: next_row(1))
                x_low(xa_hi, xa_lo, tiles_xa(g + 1), 0)
                for i in range(TT):
                    add_blocks(bb + 8 * NP - 16 + 8 * (i // 2), False, 4, 0, 4 * (i % 2))
                    if i in (0, 1):
                        next_row(i + 2)
                    if i < TT - 1:
                        x_low(xa_hi, xa_lo, tiles_xa(g + 1), i + 1)

            def lora_low(dst, n):
                dve.wait_ge(low_hi, n + 1)
                nc.vector.scalar_tensor_tensor(dst[64:P, :], bank_l[64:P, :], LORA_SCALE,
                                               dst[64:P, :].bitcast(F32), ALU.mult,
                                               ALU.subtract).then_inc(low_lo, 1)

            def phase_b(g, last):
                pb, bb, hb = prods_b(g, last), blocks_b(g), chunks_b(g)
                n0 = g * NC
                lora_low(lora_act, 2 * g)

                def product(p, r):
                    c = 2 * p + r
                    dve.wait_ge(ffn_silu, n0 + c + 1)
                    dve.wait_ge(job_done, pb + 2 * c + 3)
                    need(dve, h_lo_done, hb + c - 1)
                    nc.vector.tensor_tensor(hf[:, r, :], act_s[:, r, :], bank_c[r][:, :],
                                            ALU.mult).then_inc(h_done, 1)

                def pairs(p, beside_0=None, beside_1=None, after=None):
                    if not last and beside_0 is not None:
                        beside_0()
                    product(p, 0)
                    if not last and beside_1 is not None:
                        beside_1()
                    product(p, 1)
                    if not last and after is not None:
                        after()

                def step(p):
                    pairs(p, lambda: count_below(at, (0, 1)), lambda: (count_below(at, (2, 3)), search_move()))

                pairs(0, lambda: search_sums(g + 1, (0, 1)), lambda: (search_sums(g + 1, (2, 3)), search_start()))
                step(1)
                add_blocks(bb, True, 8, 4 * TT * g + 2 * TT)
                with dve.Fori(2, STEPS + 1) as p:
                    step(p)
                    add_blocks(bb + 8 * p - 8, False, 8, 0)
                pairs(NP - 3, lambda: search_pick((0,)), lambda: search_pick((1,)))
                add_blocks(bb + 8 * NP - 32, False, 8, 0)
                pairs(NP - 2, lambda: search_pick((2,)), lambda: search_pick((3,)))
                add_blocks(bb + 8 * NP - 24, False, 8, 0)
                pairs(NP - 1, search_end)
                add_blocks(bb + 8 * NP - 16, False, 8, 0)
                add_blocks(bb + 8 * NP - 8, False, 8, 0)
                if not last:
                    mask(0, 0)
                    mask(1, 1)
                lora_low(lora_act, 2 * g + 1)
                add_blocks(bb + 8 * NP, False, 8, 0)

            for i in range(8):
                nc.vector.memset(rank[:, i:i + 1], float(i + 1))
            nc.vector.memset(bad[:, :], 0.0)
            for t in range(TT):
                rows_here(rows_norm(0), t)
                statistics(row_x[t % 2])
                rows_to_xn(rows_norm(0), 0, t, mv[:, 0:1], rb[:, :])
                if t:
                    x_low(xa_hi, xa_lo, 0, t - 1)
            x_low(xa_hi, xa_lo, 0, TT - 1)
            phase_g(0)
            search(0)
            mask(0, 0)
            mask(1, 1)
            phase_u(0)
            with dve.Fori(1, NG) as g:
                phase_g(g)
                phase_b(g - 1, False)
                phase_u(g)
            g = NG - 1
            for t in range(TT):
                mid_rows(g, t)
                mid_to_xn(g, t)
                if t:
                    x_low(xb_hi, xb_lo, tiles_xb(g), t - 1)
            x_low(xb_hi, xb_lo, tiles_xb(g), TT - 1)
            phase_b(g, True)
            for t in range(TT):
                out_statistics(g, t)
                out_rows(g, t, t % 2, 16 * (2 * rows_out(g) + t // 2 + 1))


def kernel(**inputs):
    import numpy as np
    import concourse.bacc as bacc
    from concourse.bass_utils import run_bass_kernel_spmd

    a = {k: np.ascontiguousarray(v) for k, v in inputs.items()}
    x = a["L0_attn_x"]
    pad = NC * P - I

    def in_tiles(w, lora=None, rows=()):
        w = np.pad(w, ((0, pad), (0, 0))).reshape(NC, P, KB, P).transpose(0, 3, 2, 1).reshape(NC, P, H)
        if lora is None:
            return np.ascontiguousarray(w)
        b = np.zeros((NC, P, P), w.dtype)
        t = np.pad(lora, ((0, pad), (0, 0))).reshape(NC, P, R).transpose(0, 2, 1)
        for at in rows:
            b[:, at:at + R] = t
        return np.concatenate([w, b], 2)

    def down_tiles(w, lora=None):
        w = np.pad(w, ((0, 0), (0, pad))).reshape(2, 512, NP, 2, P).transpose(2, 0, 4, 3, 1).reshape(NC, P, H)
        if lora is None:
            return np.ascontiguousarray(w)
        b = np.zeros((NC, P, P), w.dtype)
        t = np.pad(lora, ((0, 0), (0, pad))).reshape(R, NC, P).transpose(1, 2, 0)
        for at in (0, 64):
            b[:, :, at:at + R] = t
        return np.concatenate([w, b], 2)

    a13 = np.zeros((P, KB, P), x.dtype)
    for at, name in ((0, "L0_ffn_lora_A1"), (32, "L0_ffn_lora_A3"), (64, "L0_ffn_lora_A1"),
                     (96, "L0_ffn_lora_A3")):
        a13[:, :, at:at + R] = a[name].reshape(R, KB, P).transpose(2, 1, 0)
    a13 = np.concatenate([a13.reshape(P, H), np.zeros((P, P), x.dtype)], 1)
    b2 = np.zeros((P, WX), x.dtype)
    for at in (0, 64):
        b2[at:at + R, 0:H] = a["L0_ffn_lora_B2"].T

    arrays = {
        "x": np.pad(x.reshape(TOKENS, H), ((0, TG), (0, 0))),
        "w_gate": in_tiles(a["L0_attn_w_gate"]),
        "w_up": in_tiles(a["L0_attn_w_up"]),
        "w_down": down_tiles(a["L0_attn_w_down"]),
        "w1": in_tiles(a["L0_ffn_w1"], a["L0_ffn_lora_B1"], (0, 64)),
        "w3": in_tiles(a["L0_ffn_w3"], a["L0_ffn_lora_B3"], (32, 96)),
        "w2": down_tiles(a["L0_ffn_w2"], a["L0_ffn_lora_A2"]),
        "lora_a13": a13,
        "lora_b2": b2,
    }
    nc = bacc.Bacc("TRN2", target_bir_lowering=False, num_devices=1)
    ins = {k: nc.dram_tensor(k, v.shape, mybir.dt.from_np(v.dtype), kind="ExternalInput").ap()
           for k, v in arrays.items()}
    out = nc.dram_tensor("out", (TOKENS, H), F32, kind="ExternalOutput").ap()
    ffn_sandwich(nc, **ins, out=out)
    r = run_bass_kernel_spmd(nc, [arrays], core_ids=[0])
    return r.results[0]["out"].reshape(x.shape)
```
